# Optimizing a Trainium2 kernel written in Bass

```python
import numpy as np
import jax
import jax.numpy as jnp

def _softmax(x, axis=-1):
    return jax.nn.softmax(x, axis=axis)

def _gelu(x):
    return jax.nn.gelu(x, approximate=True)

def _silu(x):
    return jax.nn.silu(x)

def _sigmoid(x):
    return jax.nn.sigmoid(x)

def _layernorm(x, axis=-1, eps=1e-05):
    m = jnp.mean(x, axis=axis, keepdims=True)
    v = jnp.var(x, axis=axis, keepdims=True)
    return (x - m) / jnp.sqrt(v + eps)

def _scatter_add(tgt, idx, src, axis=0):
    return tgt.at[idx].add(src)

def _segment_sum(src, seg, n):
    return jax.ops.segment_sum(src, seg, n)
kernel_name = 'mk_adaln_d1_jaxref_r4_f33fa8'

def setup_inputs(seed: int=0):
    np.random.seed(seed)
    _w = jnp.asarray

    def _L0_attn_setup():
        import jax, jax.numpy as jnp
        import numpy as np
        B, T, C, H = (4, 1024, 512, 16)
        Dh = C // H

        def _feature_map(x):
            return jax.nn.elu(x) + 1.0
        key = jax.random.key(seed)
        ks = jax.random.split(key, 7)
        s = 0.02
        return {'x': jax.random.normal(ks[0], (B, T, C), dtype=jnp.float32), 'cos': jax.random.uniform(ks[1], (T, Dh), dtype=jnp.float32), 'sin': jax.random.uniform(ks[2], (T, Dh), dtype=jnp.float32), 'Wq': jax.random.normal(ks[3], (C, C), dtype=jnp.float32) * s, 'Wk': jax.random.normal(ks[4], (C, C), dtype=jnp.float32) * s, 'Wv': jax.random.normal(ks[5], (C, C), dtype=jnp.float32) * s, 'Wo': jax.random.normal(ks[6], (C, C), dtype=jnp.float32) * s}
    _L0_attn_in = _L0_attn_setup()

    def _L0_ffn_setup():
        import jax, jax.numpy as jnp
        import numpy as np
        IN_F, OUT_F = (512, 512)
        N_EXPERTS, RANK, TOP_K = (8, 128, 2)
        key = jax.random.key(seed)
        k_x, k_r, k_a, k_b = jax.random.split(key, 4)
        hidden_states = jax.random.normal(k_x, (4, 1024, IN_F), dtype=jnp.float32)
        router_w = jax.random.normal(k_r, (IN_F, N_EXPERTS), dtype=jnp.float32) * IN_F ** (-0.5)
        Wa = jax.random.normal(k_a, (N_EXPERTS, IN_F, RANK), dtype=jnp.float32) * IN_F ** (-0.5)
        Wb = jax.random.normal(k_b, (N_EXPERTS, RANK, OUT_F), dtype=jnp.float32) * RANK ** (-0.5)
        return {'hidden_states': hidden_states, 'router_w': router_w, 'Wa': Wa, 'Wb': Wb}
    _L0_ffn_in = _L0_ffn_setup()
    _L0_c = _w((lambda *s: np.random.randn(*s).astype(np.float32) * 0.05)(2, 512))
    _L0_wmod = _w((lambda *s: np.random.randn(*s).astype(np.float32) * 0.05)(512, 6 * 512) * 512 ** (-0.5))
    _d = {'L0_attn_x': _L0_attn_in['x'], 'L0_attn_cos': _L0_attn_in['cos'], 'L0_attn_sin': _L0_attn_in['sin'], 'L0_attn_Wq': _L0_attn_in['Wq'], 'L0_attn_Wk': _L0_attn_in['Wk'], 'L0_attn_Wv': _L0_attn_in['Wv'], 'L0_attn_Wo': _L0_attn_in['Wo'], 'L0_ffn_router_w': _L0_ffn_in['router_w'], 'L0_ffn_Wa': _L0_ffn_in['Wa'], 'L0_ffn_Wb': _L0_ffn_in['Wb'], 'L0_c': _L0_c, 'L0_wmod': _L0_wmod}
    _x0 = _d['L0_attn_x']
    _d['L0_attn_x'] = jax.random.normal(jax.random.fold_in(jax.random.key(seed), 1), (2, 1024, 512), dtype=_x0.dtype)
    del _x0
    return _d

def reference(L0_attn_x, L0_attn_cos, L0_attn_sin, L0_attn_Wq, L0_attn_Wk, L0_attn_Wv, L0_attn_Wo, L0_ffn_router_w, L0_ffn_Wa, L0_ffn_Wb, L0_c, L0_wmod):

    def _L0_attn_ref(x, cos, sin, Wq, Wk, Wv, Wo):
        import jax, jax.numpy as jnp
        import numpy as np
        B, T, C, H = (4, 1024, 512, 16)
        Dh = C // H

        def _feature_map(x):
            return jax.nn.elu(x) + 1.0
        b, t, c = x.shape
        h, dh = (H, c // H)

        def proj(W):
            y = jnp.einsum('btc,oc->bto', x, W)
            return y.reshape(b, t, h, dh).transpose(0, 2, 1, 3)
        q = _feature_map(proj(Wq))
        k = _feature_map(proj(Wk))
        v = proj(Wv)
        kv = jnp.einsum('bhtd,bhte->bhde', k, v)
        z = 1.0 / (jnp.einsum('bhtd,bhd->bht', q, k.sum(axis=2)) + 1e-06)
        out = jnp.einsum('bhtd,bhde,bht->bhte', q, kv, z)
        out = out.transpose(0, 2, 1, 3).reshape(b, t, c)
        return jnp.einsum('btc,oc->bto', out, Wo)

    def _L0_ffn_ref(hidden_states, router_w, Wa, Wb):
        import jax, jax.numpy as jnp
        import numpy as np
        IN_F, OUT_F = (512, 512)
        N_EXPERTS, RANK, TOP_K = (8, 128, 2)
        B, S, D = hidden_states.shape
        x = hidden_states.reshape(-1, D)
        norm = jnp.maximum(jnp.linalg.norm(x, axis=-1, keepdims=True), 1e-12)
        router_logits = x / norm @ router_w
        routing_weights = jax.nn.softmax(router_logits.astype(jnp.float32), axis=-1)
        rw, selected_experts = jax.lax.top_k(routing_weights, TOP_K)
        rw = rw / jnp.sum(rw, axis=-1, keepdims=True)
        rw = rw.astype(hidden_states.dtype)
        combine = jnp.sum(jax.nn.one_hot(selected_experts, N_EXPERTS, dtype=rw.dtype) * rw[..., None], axis=1)
        out = jnp.zeros((x.shape[0], OUT_F), dtype=hidden_states.dtype)
        for e in range(N_EXPERTS):
            out = out + combine[:, e, None] * (x @ Wa[e] @ Wb[e])
        return out.reshape(B, S, OUT_F)
    x = L0_attn_x
    mod = (_silu(L0_c) @ L0_wmod).reshape(L0_c.shape[0], 6, 1, -1)
    sa, ca, ga, sb, cb, gb = (mod[:, 0], mod[:, 1], mod[:, 2], mod[:, 3], mod[:, 4], mod[:, 5])
    ga = (2 * (ga >= 0) - 1) * jnp.maximum(jnp.abs(ga), 0.25)
    gb = (2 * (gb >= 0) - 1) * jnp.maximum(jnp.abs(gb), 0.25)
    h = _layernorm(x, axis=-1) * (1 + ca) + sa
    x = x + ga * _L0_attn_ref(h, L0_attn_cos, L0_attn_sin, L0_attn_Wq, L0_attn_Wk, L0_attn_Wv, L0_attn_Wo)
    h = _layernorm(x, axis=-1) * (1 + cb) + sb
    x = x + gb * _L0_ffn_ref(h, L0_ffn_router_w, L0_ffn_Wa, L0_ffn_Wb)
    return x

_drawn_inputs = setup_inputs


def setup_inputs(seed=0):
    import zlib

    import numpy as np

    out = dict(_drawn_inputs(seed))
    spreads = {}
    factors = {'L0_attn_Wq': 8.0, 'L0_attn_Wk': 8.0, 'L0_attn_Wv': 6.904, 'L0_attn_Wo': 7.57}
    for name, (base, spread) in spreads.items():
        noise = np.random.default_rng([zlib.crc32(name.encode()), seed]).standard_normal(out[name].shape)
        drawn = base * np.exp(spread * noise) if base else spread * noise
        out[name] = jnp.asarray(drawn.astype(out[name].dtype))
    for name, factor in factors.items():
        out[name] = (out[name] * factor).astype(out[name].dtype)
    return out
```

```python
from contextlib import ExitStack

import concourse.bass as bass
from concourse import mybir

ALU = mybir.AluOpType
ACT = mybir.ActivationFunctionType
AX = mybir.AxisListType
F32 = mybir.dt.float32
F32R = mybir.dt.float32r
U32 = mybir.dt.uint32

P = 128
LN_EPS = 1e-5
DEN_EPS = 1e-6
NORM_FLOOR = 1e-12
GATE_FLOOR = 0.25
KB = 1024
SA, CA, GA, SB, CB, GB = range(6)
MOD_ORDER = [CA, SA, GA, SB, CB, GB]
Q, K, V = range(3)


def adaln_block(nc, x, c_cols, wq, wk, wv, wo, router, wa, wb, wmod, mod_rows, out):
    TOK, C = x.shape
    B = c_cols.shape[2]
    E, R, _ = wb.shape
    KC = C // P
    NT = TOK // P
    TB = NT // B
    DH = 32
    H = C // DH
    NB = E * R // C
    EPB = E // NB
    assert C == 512 and R == P and E == 8 and NT * P == TOK and TB * B == NT and TB >= 4

    x_t = x.rearrange("(n p) c -> p n c", p=P)
    out_t = out.rearrange("(n p) c -> p n c", p=P)

    def chunked(w):
        return w.rearrange("(k p) n -> p k n", p=P)

    BASE = 16512
    ROW = C * 4
    WQKV_AT = BASE
    WO_AT = WQKV_AT + 2 * 3 * KC * ROW
    XQ_AT = WO_AT + KC * ROW
    U_AT = XQ_AT + NT * ROW
    WA_AT = U_AT + 2 * B * KC * ROW
    MODS_AT = WA_AT + 2 * KC * NB * ROW
    STAGE_AT = MODS_AT + 6 * B * ROW
    SMALL_AT = STAGE_AT + 14 * ROW

    def at(name, shape, dt, offset):
        return nc.alloc_sbuf_tensor_at(name, shape, dt, offset=offset)

    w_hi = at("w_hi", [P, 3, KC, C], F32R, WQKV_AT)
    w_lo = at("w_lo", [P, 3, KC, C], F32R, WQKV_AT + 3 * KC * ROW)
    wb_hi = at("wb_hi", [P, E, C], F32R, WQKV_AT)
    wb_lo = at("wb_lo", [P, E, C], F32R, WQKV_AT + E * ROW)
    wb_raw = at("wb_raw", [P, E, C], F32, WQKV_AT + 2 * E * ROW)
    wo_f = at("wo_f", [P, KC, C], F32, WO_AT)
    sT_hi = at("sT_hi", [P, E, P], F32R, WO_AT)
    sT_lo = at("sT_lo", [P, E, P], F32R, WO_AT + 2 * ROW)
    xq = at("xq", [P, NT, C], F32, XQ_AT)
    m_hi = at("m_hi", [P, B, KC, C], F32R, U_AT)
    m_lo = at("m_lo", [P, B, KC, C], F32R, U_AT + B * KC * ROW)
    wa_hi = at("wa_hi", [P, KC, E * R], F32R, WA_AT)
    wa_lo = at("wa_lo", [P, KC, E * R], F32R, WA_AT + KC * NB * ROW)
    wmod_raw = [at(f"wmod_raw{n}", [P, KC, C], F32, U_AT + n * KC * ROW) for n in range(6)]
    raw = {
        Q: at("wq_raw", [P, KC, C], F32, U_AT),
        K: at("wk_raw", [P, KC, C], F32, U_AT + 6 * KC * ROW),
        V: at("wv_raw", [P, KC, C], F32, U_AT + 7 * KC * ROW),
    }
    wa_raw = at("wa_raw", [P, KC, E * R], F32, U_AT + 2 * KC * ROW)
    mods = at("mods", [P, 6, B, C], F32, MODS_AT)

    def stage(name, n, dt=F32, rows=1, shape=None):
        return at(name, shape or [P, rows * C], dt, STAGE_AT + n * ROW)

    h = stage("h", 0)
    hT_hi = stage("hT_hi", 1, F32R)
    hT_lo = stage("hT_lo", 2, F32R)
    exp_k, relu_k = stage("exp_k", 3), stage("relu_k", 4)
    exp_q, relu_q = stage("exp_q", 5), stage("relu_q", 6)
    k_sb, v_sb = stage("k_sb", 7), stage("v_sb", 8)
    k_acc = stage("k_acc", 9)
    kv_sb = stage("kv_sb", 10)
    m_f = [stage("m_f0", 11), stage("m_f1", 12)]
    mod_row = [stage("mod_row0", 10), stage("mod_row1", 11)]
    sign_row, mag_row = stage("sign_row", 12), stage("mag_row", 13)
    qzT_hi, qzT_lo = stage("qzT_hi", 3, F32R), stage("qzT_lo", 4, F32R)
    s_sb = stage("s_sb", 7, rows=NB)
    q_ksum = at("q_ksum", [P, C], F32, MODS_AT + (SA * B + 0) * ROW)
    qz = at("qz", [P, C], F32, MODS_AT + (SA * B + 1) * ROW)
    square = at("square", [P, C], F32, MODS_AT + (GA * B + 0) * ROW)
    ffn = at("ffn", [P, C], F32, MODS_AT + (GA * B + 1) * ROW)

    small_end = [SMALL_AT]

    def small(name, shape, dt=F32):
        n = 1
        for d in shape[1:]:
            n *= d
        t = at(name, shape, dt, small_end[0])
        small_end[0] += -(-n * 4 // 32) * 32
        return t

    ident = small("ident", [P, P])
    ones = small("ones", [P, P])
    head_mask = small("head_mask", [P, P])
    router_raw = small("router_raw", [P, KC, E])
    router_2 = small("router_2", [P, KC, 2 * E], F32R)
    c_sb = small("c_sb", [P, KC, B])
    exp_c = small("exp_c", [P, KC, B])
    silu_c = small("silu_c", [P, KC, B])
    minus_half = small("minus_half", [P, 1])
    expert_no = small("expert_no", [P, E])
    bn6 = small("bn6", [P, 6])
    mean_var = small("mean_var", [P, 2])
    var_eps = small("var_eps", [P, 1])
    rstd = small("rstd", [P, 1])
    den = small("den", [P, H])
    den_eps = small("den_eps", [P, H])
    z = small("z", [P, H])
    sq_sum = small("sq_sum", [P, 1])
    sq_floor = small("sq_floor", [P, 1])
    inv_norm = small("inv_norm", [P, 1])
    logit_lo = small("logit_lo", [P, E])
    logits = small("logits", [P, E])
    top = small("top", [P, 8])
    top_at = small("top_at", [P, 8], U32)
    top_at_f = small("top_at_f", [P, 2])
    gap = small("gap", [P, 1])
    ratio = small("ratio", [P, 1])
    ratio_1 = small("ratio_1", [P, 1])
    weight = small("weight", [P, 2])
    combine_0 = small("combine_0", [P, E])
    combine_1 = small("combine_1", [P, E])
    combine = small("combine", [P, E])

    with ExitStack() as ctx:
        banks = [ctx.enter_context(nc.psum_tensor(f"bank{n}", [P, C], F32)) for n in range(8)]
        k_ps, v_ps, q_ps, hT_ps, kv_ps, ksum_ps = banks[:6]
        m_ps = banks[6:8]
        up_ps = banks[0:2]
        attn_ps, t_ps, ffn_ps, logit_ps = banks[2:6]
        sT_ps = banks[6:8]

        def sem(name):
            return ctx.enter_context(nc.semaphore(name))

        c_in, wo_in, router_in, wa_in, wb_in = (sem(s) for s in ("c_in", "wo_in", "router_in", "wa_in", "wb_in"))
        wmod_in = [sem(f"wmod_in{n}") for n in range(6)]
        w_in = {j: sem(f"w_in{j}") for j in (Q, K, V)}
        x_in = [sem(f"x_in{n}") for n in range(3)]
        x_again = sem("x_again")
        out_done = sem("out_done")
        const_step, const_ready, ident_ready = sem("const_step"), sem("const_ready"), sem("ident_ready")
        c_exp, silu_step, silu_ready = sem("c_exp"), sem("silu_step"), sem("silu_ready")
        mod_mm, mod_row_ready, gate_step = sem("mod_mm"), sem("mod_row_ready"), sem("gate_step")
        mod_stored, mod_spread = sem("mod_stored"), sem("mod_spread")
        w_hi_ready, w_lo_ready = sem("w_hi_ready"), sem("w_lo_ready")
        router_hi_ready, router_ready = sem("router_hi_ready"), sem("router_ready")
        wa_hi_ready, wa_ready = sem("wa_hi_ready"), sem("wa_ready")
        wb_hi_ready, wb_ready = sem("wb_hi_ready"), sem("wb_ready")
        bn_ready, stats_ready, var_ready, rstd_ready = (sem(s) for s in ("bn_ready", "stats_ready", "var_ready", "rstd_ready"))
        scaled_ready, h_ready = sem("scaled_ready"), sem("h_ready")
        h_transposed, hT_hi_ready, hT_lo_ready = (sem(s) for s in ("h_transposed", "hT_hi_ready", "hT_lo_ready"))
        k_mm, v_mm, q_mm, kv_mm = (sem(s) for s in ("k_mm", "v_mm", "q_mm", "kv_mm"))
        k_parts, q_parts = sem("k_parts"), sem("q_parts")
        k_ready, v_ready, q_ready, k_added = (sem(s) for s in ("k_ready", "v_ready", "q_ready", "k_added"))
        ksum_mm, ksum_ready, kv_ready = sem("ksum_mm"), sem("ksum_ready"), sem("kv_ready")
        m_mm, m_gated, m_hi_ready, m_ready = sem("m_mm"), sem("m_gated"), sem("m_hi_ready"), sem("m_ready")
        q_ksum_ready, den_step, qz_ready, qz_transposed = (sem(s) for s in ("q_ksum_ready", "den_step", "qz_ready", "qz_transposed"))
        qzT_hi_ready, qzT_lo_ready = sem("qzT_hi_ready"), sem("qzT_lo_ready")
        attn_mm, x1_ready = sem("attn_mm"), sem("x1_ready")
        sq_ready, sq_floored, norm_ready = sem("sq_ready"), sem("sq_floored"), sem("norm_ready")
        logit_mm, logits_ready, top2_step, ratio_ready = (sem(s) for s in ("logit_mm", "logits_ready", "top2_step", "ratio_ready"))
        up_mm, s_ready, s_transposed = sem("up_mm"), sem("s_ready"), sem("s_transposed")
        sT_hi_ready, sT_lo_ready = sem("sT_hi_ready"), sem("sT_lo_ready")
        ffn_mm, ffn_ready, out_ready = sem("ffn_mm"), sem("ffn_ready"), sem("out_ready")

        sp_passed, pool_passed, dve_passed = sem("sp_passed"), sem("pool_passed"), sem("dve_passed")

        def wait(eng, s, value):
            if not (isinstance(value, int) and value <= 0):
                eng.wait_ge(s, value)

        def wait_apart(eng, passed, s, value):
            wait(eng, s, value)
            if not isinstance(value, int):
                eng.sem_inc(passed, 1)

        def cols(j, width=P):
            return slice(j * width, (j + 1) * width)

        def f32(t):
            return t.bitcast(F32)

        CONSTANTS = 3 + P // DH + E
        TOP2 = 10

        block = ctx.enter_context(nc.Block())

        @block.sync
        def _(sp):
            def load_wmod(n):
                j = MOD_ORDER[n]
                sp.dma_start(wmod_raw[n][:], chunked(wmod[:, cols(j, C)])).then_inc(wmod_in[n], 16)

            sp.dma_start(c_sb[:], c_cols).then_inc(c_in, 16)
            load_wmod(0)
            load_wmod(1)
            sp.dma_start(xq[:, 0, :], x_t[:, 0, :]).then_inc(x_in[0], 16)
            sp.dma_start(raw[K][:], chunked(wk)).then_inc(w_in[K], 16)
            sp.dma_start(raw[V][:], chunked(wv)).then_inc(w_in[V], 16)
            sp.wait_ge(mod_mm, 1)
            sp.dma_start(raw[Q][:], chunked(wq)).then_inc(w_in[Q], 16)
            sp.dma_start(xq[:, 1:TB, :], x_t[:, 1:TB, :]).then_inc(x_in[1], 16)
            for n in range(2, 6):
                load_wmod(n)
            sp.dma_start(xq[:, TB:NT, :], x_t[:, TB:NT, :]).then_inc(x_in[2], 16)
            sp.dma_start(wo_f[:], chunked(wo)).then_inc(wo_in, 16)
            sp.dma_start(router_raw[:], router).then_inc(router_in, 16)
            sp.wait_ge(mod_mm, 6)
            sp.dma_start(wa_raw[:], chunked(wa)).then_inc(wa_in, 16)
            sp.wait_ge(q_mm, NT)
            sp.dma_start(wb_raw[:], wb.rearrange("e r c -> r e c")).then_inc(wb_in, 16)

            def reload_x(n):
                sp.wait_ge(qz_ready, n + 1)
                sp.dma_start(xq[:, n, :], x_t[:, n, :]).then_inc(x_again, 16)
                wait_apart(sp, sp_passed, x_again, 16 * (n + 1))

            def store(n):
                sp.wait_ge(out_ready, n + 1)
                sp.dma_start(out_t[:, n, :], xq[:, n, :]).then_inc(out_done, 16)

            LAG = 4
            with sp.Fori(0, LAG) as n:
                reload_x(n)
            with sp.Fori(LAG, NT) as n:
                reload_x(n)
                store(n - LAG)
            with sp.Fori(NT - LAG, NT) as n:
                store(n)
            sp.wait_ge(out_done, 16 * NT)

        @block.gpsimd
        def _(pool):
            nc.gpsimd.memset(ident[:], 1.0).then_inc(const_step, 1)
            pool.wait_ge(const_step, 1)
            nc.gpsimd.affine_select(out=ident[:], in_=ident[:], compare_op=ALU.is_equal, fill=0.0, base=0,
                                    pattern=[[-1, P]], channel_multiplier=1).then_inc(ident_ready, 1)
            pool.wait_ge(ident_ready, 1)
            pool.wait_ge(const_ready, CONSTANTS)

            def spread_mod(n):
                j = MOD_ORDER[n]
                pool.wait_ge(mod_row_ready, n + 1)
                pool.dma_start(mod_rows[j], mod_row[n % 2][0:B, :]).then_inc(mod_stored, 16)
                pool.wait_ge(mod_stored, 16 * (n + 1))
                pool.dma_start(mods[:, j, :, :], mod_rows[j].unsqueeze(0).broadcast_to((P, B, C))).then_inc(mod_spread, 16)

            def inverse_std(m):
                pool.wait_ge(stats_ready, m + 1)
                wait_apart(pool, pool_passed, h_ready, m)
                nc.gpsimd.tensor_scalar(var_eps[:], mean_var[:, 1:2], LN_EPS, None, ALU.add).then_inc(var_ready, 1)
                pool.wait_ge(var_ready, m + 1)
                nc.gpsimd.tensor_tensor(rstd[:], var_eps[:], minus_half[:], ALU.pow).then_inc(rstd_ready, 1)

            spread_mod(0)
            spread_mod(1)
            inverse_std(0)
            pool.wait_ge(mod_spread, 32)

            def add_k(i, first):
                pool.wait_ge(k_ready, i + 1)
                if first:
                    wait(pool, ksum_mm, i // TB)
                    nc.gpsimd.tensor_copy(k_acc[:], k_sb[:]).then_inc(k_added, 1)
                else:
                    pool.wait_ge(k_added, i)
                    nc.gpsimd.tensor_tensor(k_acc[:], k_acc[:], k_sb[:], ALU.add).then_inc(k_added, 1)

            def split_wa(t):
                k, half = t // NB, t % NB
                src = wa_raw[:, k, cols(half, C)]
                nc.gpsimd.tensor_copy(wa_hi[:, k, cols(half, C)], src).then_inc(wa_hi_ready, 1)
                pool.wait_ge(wa_hi_ready, t + 1)
                nc.gpsimd.tensor_tensor(wa_lo[:, k, cols(half, C)], src, f32(wa_hi[:, k, cols(half, C)]),
                                        ALU.subtract).then_inc(wa_ready, 1)

            assert KC * NB == TB
            for b in range(B):
                i = b * TB
                inverse_std(i + 1)
                add_k(i, True)
                if b == 0:
                    for n in range(2, 6):
                        spread_mod(n)
                    pool.wait_ge(wa_in, 16)
                    pool.wait_ge(w_lo_ready, 3)
                with pool.Fori(1, TB - 1) as t:
                    inverse_std(b * TB + t + 1)
                    add_k(b * TB + t, False)
                i = b * TB + TB - 1
                if i + 1 < NT:
                    inverse_std(i + 1)
                add_k(i, False)
                if b == 0:
                    for t in range(TB):
                        split_wa(t)

            def inverse_norm(n):
                pool.wait_ge(sq_ready, n + 1)
                wait_apart(pool, pool_passed, logits_ready, n)
                nc.gpsimd.tensor_scalar(sq_floor[:], sq_sum[:], NORM_FLOOR * NORM_FLOOR, None, ALU.max).then_inc(sq_floored, 1)
                pool.wait_ge(sq_floored, n + 1)
                nc.gpsimd.tensor_tensor(inv_norm[:], sq_floor[:], minus_half[:], ALU.pow).then_inc(norm_ready, 1)

            def add_ffn(n):
                pool.wait_ge(ffn_ready, n + 1)
                nc.gpsimd.tensor_tensor(xq[:, n, :], xq[:, n, :], ffn[:], ALU.add).then_inc(out_ready, 1)

            def step(i, has_prev, has_next):
                if has_next:
                    inverse_std(NT + i + 1)
                    inverse_norm(i + 1)
                if has_prev:
                    add_ffn(i - 1)

            inverse_std(NT)
            inverse_norm(0)
            step(0, False, True)
            with pool.Fori(1, NT - 3) as i:
                step(i, True, True)
            for i in range(NT - 3, NT):
                step(i, True, i + 1 < NT)
            add_ffn(NT - 1)

        @block.scalar
        def _(act):
            act.wait_ge(c_in, 16)
            nc.scalar.activation(exp_c[:], c_sb[:], ACT.Exp, scale=-1.0).then_inc(c_exp, 1)

            def split_w(j, n):
                act.wait_ge(w_in[j], 16)
                nc.scalar.activation(w_hi[:, j, :, :], raw[j][:], ACT.Copy).then_inc(w_hi_ready, 1)

            def split_hT(m):
                act.wait_ge(h_transposed, m + 1)
                nc.scalar.activation(hT_hi[:], hT_ps[:], ACT.Copy).then_inc(hT_hi_ready, 1)

            split_w(K, 0)
            split_w(V, 1)
            split_hT(0)
            split_w(Q, 2)

            def tile(i, has_next):
                act.wait_ge(k_mm, i + 1)
                wait(act, k_ready, i)
                nc.scalar.activation(exp_k[:], k_ps[:], ACT.Exp)
                nc.scalar.activation(relu_k[:], k_ps[:], ACT.Relu).then_inc(k_parts, 1)
                act.wait_ge(v_mm, i + 1)
                wait(act, kv_mm, i)
                nc.scalar.activation(v_sb[:], v_ps[:], ACT.Copy).then_inc(v_ready, 1)
                act.wait_ge(q_mm, i + 1)
                wait(act, q_ready, i)
                nc.scalar.activation(exp_q[:], q_ps[:], ACT.Exp)
                nc.scalar.activation(relu_q[:], q_ps[:], ACT.Relu).then_inc(q_parts, 1)
                if has_next:
                    split_hT(i + 1)

            for b in range(B):
                tile(b * TB, True)
                with act.Fori(1, TB - 1) as t:
                    tile(b * TB + t, True)
                tile(b * TB + TB - 1, b + 1 < B)
                act.wait_ge(ksum_mm, b + 1)
                act.wait_ge(h_ready, (b + 1) * TB)
                nc.scalar.activation(mods[:, CA, b, :], ksum_ps[:], ACT.Copy).then_inc(ksum_ready, 1)

            def split_qz(n):
                act.wait_ge(qz_transposed, n + 1)
                wait(act, attn_mm, n)
                nc.scalar.activation(qzT_hi[:], t_ps[:], ACT.Copy).then_inc(qzT_hi_ready, 1)

            def square_sum(n):
                act.wait_ge(h_ready, NT + n + 1)
                wait(act, norm_ready, n)
                nc.scalar.activation(square[:], h[:], ACT.Square, accum_out=sq_sum[:]).then_inc(sq_ready, 1)

            def step(i, has_next, has_second):
                act.wait_ge(top2_step, TOP2 * i + 4)
                nc.scalar.activation(ratio[:], gap[:], ACT.Exp).then_inc(ratio_ready, 1)
                if has_second:
                    split_qz(i + 2)
                if has_next:
                    square_sum(i + 1)
                    split_hT(NT + i + 1)
                act.wait_ge(s_transposed, i + 1)
                for j in range(NB):
                    last = nc.scalar.activation(sT_hi[:, j * EPB:(j + 1) * EPB, :], sT_ps[j][:], ACT.Copy)
                last.then_inc(sT_hi_ready, 1)

            split_qz(0)
            split_qz(1)
            square_sum(0)
            split_hT(NT)
            act.wait_ge(wb_in, 16)
            for g in range(2):
                e = slice(g * E // 2, (g + 1) * E // 2)
                nc.scalar.activation(wb_hi[:, e, :], wb_raw[:, e, :], ACT.Copy).then_inc(wb_hi_ready, 1)
            step(0, True, True)
            with act.Fori(1, NT - 3) as i:
                step(i, True, True)
            for i in range(NT - 3, NT):
                step(i, i + 1 < NT, i + 2 < NT)

        @block.vector
        def _(dve):
            nc.vector.memset(head_mask[:], 0.0).then_inc(const_ready, 1)
            dve.wait_ge(const_ready, 1)
            for j in range(P // DH):
                nc.vector.memset(head_mask[cols(j, DH), cols(j, DH)], 1.0).then_inc(const_ready, 1)
            nc.vector.memset(ones[:], 1.0).then_inc(const_ready, 1)
            nc.vector.memset(minus_half[:], -0.5).then_inc(const_ready, 1)
            for e in range(E):
                nc.vector.memset(expert_no[:, e:e + 1], float(e)).then_inc(const_ready, 1)
            dve.wait_ge(const_ready, CONSTANTS)
            dve.wait_ge(c_exp, 1)
            nc.vector.tensor_scalar(exp_c[:], exp_c[:], 1.0, None, ALU.add).then_inc(silu_step, 1)
            dve.wait_ge(silu_step, 1)
            nc.vector.reciprocal(exp_c[:], exp_c[:]).then_inc(silu_step, 1)
            dve.wait_ge(silu_step, 2)
            nc.vector.tensor_tensor(silu_c[:], exp_c[:], c_sb[:], ALU.mult).then_inc(silu_ready, 1)

            def mod_rows_out(n):
                j = MOD_ORDER[n]
                src, dst = m_ps[n % 2][0:B, :], mod_row[n % 2][0:B, :]
                dve.wait_ge(mod_mm, n + 1)
                wait(dve, mod_stored, 16 * (n - 1))
                if j in (GA, GB):
                    g = 3 * (0 if j == GA else 1)
                    sign, mag = sign_row[0:B, :], mag_row[0:B, :]
                    nc.vector.tensor_scalar(sign, src, 0.0, 2.0, ALU.is_ge, ALU.mult).then_inc(gate_step, 1)
                    dve.wait_ge(gate_step, g + 1)
                    nc.vector.tensor_scalar(sign, sign, -1.0, None, ALU.add).then_inc(gate_step, 1)
                    dve.wait_ge(gate_step, g + 2)
                    nc.vector.tensor_tensor(mag, src, sign, ALU.mult).then_inc(gate_step, 1)
                    dve.wait_ge(gate_step, g + 3)
                    nc.vector.scalar_tensor_tensor(out=dst, in0=mag, scalar=GATE_FLOOR, in1=sign, op0=ALU.max,
                                                   op1=ALU.mult).then_inc(mod_row_ready, 1)
                else:
                    nc.vector.tensor_scalar(dst, src, 1.0 if j in (CA, CB) else 0.0, None,
                                            ALU.add).then_inc(mod_row_ready, 1)

            def statistics(m, src):
                nc.vector.bn_stats(out=bn6[:], in_=src).then_inc(bn_ready, 1)
                dve.wait_ge(bn_ready, m + 1)
                wait_apart(dve, dve_passed, rstd_ready, m)
                nc.vector.bn_aggr(out=mean_var[:], in_=bn6[:]).then_inc(stats_ready, 1)
                dve.wait_ge(stats_ready, m + 1)

            def modulate(m, src, scale, shift):
                wait(dve, h_transposed, m)
                nc.vector.scalar_tensor_tensor(out=h[:], in0=src, scalar=mean_var[:, 0:1], in1=scale,
                                               op0=ALU.subtract, op1=ALU.mult).then_inc(scaled_ready, 1)
                dve.wait_ge(scaled_ready, m + 1)
                dve.wait_ge(rstd_ready, m + 1)
                nc.vector.scalar_tensor_tensor(out=h[:], in0=h[:], scalar=rstd[:, 0:1], in1=shift,
                                               op0=ALU.mult, op1=ALU.add).then_inc(h_ready, 1)

            def rest_of_hT(m):
                dve.wait_ge(hT_hi_ready, m + 1)
                nc.vector.tensor_tensor(hT_lo[:], hT_ps[:], f32(hT_hi[:]), ALU.subtract).then_inc(hT_lo_ready, 1)

            def rest_of_w(j, n):
                dve.wait_ge(w_hi_ready, n + 1)
                nc.vector.tensor_tensor(w_lo[:, j, :, :], raw[j][:], f32(w_hi[:, j, :, :]),
                                        ALU.subtract).then_inc(w_lo_ready, 1)

            mod_rows_out(0)
            mod_rows_out(1)
            dve.wait_ge(x_in[0], 16)
            statistics(0, xq[:, 0, :])
            rest_of_w(K, 0)
            dve.wait_ge(mod_spread, 32)
            modulate(0, xq[:, 0, :], mods[:, CA, 0, :], mods[:, SA, 0, :])
            rest_of_w(V, 1)
            rest_of_hT(0)
            rest_of_w(Q, 2)

            def tile(i, next_b):
                if next_b is not None:
                    statistics(i + 1, xq[:, i + 1, :])
                    modulate(i + 1, xq[:, i + 1, :], mods[:, CA, next_b, :], mods[:, SA, next_b, :])
                dve.wait_ge(k_parts, i + 1)
                wait(dve, k_added, i)
                wait(dve, kv_mm, i)
                nc.vector.scalar_tensor_tensor(out=k_sb[:], in0=exp_k[:], scalar=1.0, in1=relu_k[:],
                                               op0=ALU.min, op1=ALU.add).then_inc(k_ready, 1)
                dve.wait_ge(q_parts, i + 1)
                nc.vector.scalar_tensor_tensor(out=xq[:, i, :], in0=exp_q[:], scalar=1.0, in1=relu_q[:],
                                               op0=ALU.min, op1=ALU.add).then_inc(q_ready, 1)
                if next_b is not None:
                    rest_of_hT(i + 1)

            def join(b):
                dve.wait_ge(kv_mm, (b + 1) * TB)
                wait(dve, m_mm, b * KC)
                nc.vector.tensor_tensor(kv_sb[:].rearrange("p (j e) -> p j e", e=P),
                                        kv_ps[:].rearrange("p (j e) -> p j e", e=P),
                                        head_mask[:].unsqueeze(1).broadcast_to((P, KC, P)),
                                        ALU.mult).then_inc(kv_ready, 1)
                for j in range(KC):
                    n = b * KC + j
                    dve.wait_ge(m_mm, n + 1)
                    nc.vector.tensor_tensor(m_f[n % 2][:], m_ps[n % 2][:], mods[:, GA, b, :],
                                            ALU.mult).then_inc(m_gated, 1)
                    dve.wait_ge(m_gated, n + 1)
                    nc.vector.tensor_copy(m_hi[:, b, j, :], m_f[n % 2][:]).then_inc(m_hi_ready, 1)
                    dve.wait_ge(m_hi_ready, n + 1)
                    nc.vector.tensor_tensor(m_lo[:, b, j, :], m_f[n % 2][:], f32(m_hi[:, b, j, :]),
                                            ALU.subtract).then_inc(m_ready, 1)

            for b in range(B):
                if b == 0:
                    dve.wait_ge(x_in[1], 16)
                tile(b * TB, b)
                if b == 0:
                    for n in range(2, 6):
                        mod_rows_out(n)
                    dve.wait_ge(router_in, 16)
                    nc.vector.tensor_copy(router_2[:, :, 0:E], router_raw[:]).then_inc(router_hi_ready, 1)
                    dve.wait_ge(router_hi_ready, 1)
                    nc.vector.tensor_tensor(router_2[:, :, E:2 * E], router_raw[:], f32(router_2[:, :, 0:E]),
                                            ALU.subtract).then_inc(router_ready, 1)
                with dve.Fori(1, TB - 1) as t:
                    tile(b * TB + t, b)
                if b == 0:
                    dve.wait_ge(x_in[2], 16)
                tile(b * TB + TB - 1, b + 1 if b + 1 < B else None)
                if b == 0:
                    dve.wait_ge(mod_spread, 16 * 6)
                    dve.wait_ge(wa_ready, TB)
                join(b)

            def normalise_q(n):
                ksum = mods[:, CA, n // TB, :]
                wait(dve, q_ksum_ready, n)
                nc.vector.tensor_tensor(q_ksum[:], xq[:, n, :], ksum, ALU.mult).then_inc(q_ksum_ready, 1)
                dve.wait_ge(q_ksum_ready, n + 1)
                nc.vector.tensor_reduce(den[:], q_ksum[:].rearrange("p (h d) -> p h d", d=DH), AX.X,
                                        ALU.add).then_inc(den_step, 1)
                dve.wait_ge(den_step, 3 * n + 1)
                nc.vector.tensor_scalar(den_eps[:], den[:], DEN_EPS, None, ALU.add).then_inc(den_step, 1)
                dve.wait_ge(den_step, 3 * n + 2)
                nc.vector.reciprocal(z[:], den_eps[:]).then_inc(den_step, 1)
                dve.wait_ge(den_step, 3 * n + 3)
                wait(dve, qz_transposed, n)
                nc.vector.tensor_tensor(qz[:].rearrange("p (h d) -> p h d", d=DH),
                                        xq[:, n, :].rearrange("p (h d) -> p h d", d=DH),
                                        z[:].unsqueeze(2).broadcast_to((P, H, DH)), ALU.mult).then_inc(qz_ready, 1)

            def rest_of_qz(n):
                dve.wait_ge(qzT_hi_ready, n + 1)
                nc.vector.tensor_tensor(qzT_lo[:], t_ps[:], f32(qzT_hi[:]), ALU.subtract).then_inc(qzT_lo_ready, 1)

            def add_attention(n):
                dve.wait_ge(attn_mm, n + 1)
                dve.wait_ge(x_again, 16 * (n + 1))
                nc.vector.tensor_tensor(xq[:, n, :], xq[:, n, :], attn_ps[:], ALU.add).then_inc(x1_ready, 1)
                dve.wait_ge(x1_ready, n + 1)

            def norm_2(n):
                b = n // TB
                statistics(NT + n, xq[:, n, :])
                wait(dve, sq_ready, n)
                modulate(NT + n, xq[:, n, :], mods[:, CB, b, :], mods[:, SB, b, :])

            def top2(n):
                base = TOP2 * n
                dve.wait_ge(logit_mm, n + 1)
                dve.wait_ge(norm_ready, n + 1)
                nc.vector.tensor_scalar(logit_lo[:], logit_ps[:, E:2 * E], inv_norm[:, 0:1], None,
                                        ALU.mult).then_inc(top2_step, 1)
                dve.wait_ge(top2_step, base + 1)
                nc.vector.scalar_tensor_tensor(out=logits[:], in0=logit_ps[:, 0:E], scalar=inv_norm[:, 0:1],
                                               in1=logit_lo[:], op0=ALU.mult, op1=ALU.add).then_inc(logits_ready, 1)
                wait_apart(dve, dve_passed, logits_ready, n + 1)
                nc.vector.max(out=top[:], in_=logits[:]).then_inc(top2_step, 1)
                wait_apart(dve, dve_passed, top2_step, base + 2)
                nc.vector.max_index(top_at[:], top[:], logits[:]).then_inc(top2_step, 1)
                dve.wait_ge(top2_step, base + 3)
                nc.vector.tensor_tensor(gap[:], top[:, 1:2], top[:, 0:1], ALU.subtract).then_inc(top2_step, 1)
                nc.vector.tensor_copy(top_at_f[:], top_at[:, 0:2]).then_inc(top2_step, 1)
                dve.wait_ge(ratio_ready, n + 1)
                nc.vector.tensor_scalar(ratio_1[:], ratio[:], 1.0, None, ALU.add).then_inc(top2_step, 1)
                dve.wait_ge(top2_step, base + 6)
                nc.vector.reciprocal(weight[:, 0:1], ratio_1[:]).then_inc(top2_step, 1)
                dve.wait_ge(top2_step, base + 7)
                nc.vector.tensor_tensor(weight[:, 1:2], ratio[:], weight[:, 0:1], ALU.mult).then_inc(top2_step, 1)
                dve.wait_ge(top2_step, base + 8)
                nc.vector.tensor_scalar(combine_0[:], expert_no[:], top_at_f[:, 0:1], weight[:, 0:1],
                                        ALU.is_equal, ALU.mult)
                nc.vector.tensor_scalar(combine_1[:], expert_no[:], top_at_f[:, 1:2], weight[:, 1:2],
                                        ALU.is_equal, ALU.mult).then_inc(top2_step, 1)
                dve.wait_ge(top2_step, base + 9)
                nc.vector.tensor_tensor(combine[:], combine_0[:], combine_1[:], ALU.add).then_inc(top2_step, 1)
                dve.wait_ge(top2_step, base + 10)

            def scale_up(n):
                dve.wait_ge(up_mm, n + 1)
                wait(dve, s_transposed, n)
                for j in range(NB):
                    last = nc.vector.tensor_tensor(
                        s_sb[:, cols(j, C)].rearrange("p (e r) -> p e r", r=R),
                        up_ps[j][:].rearrange("p (e r) -> p e r", r=R),
                        combine[:, j * EPB:(j + 1) * EPB].unsqueeze(2).broadcast_to((P, EPB, R)), ALU.mult)
                last.then_inc(s_ready, 1)

            def rest_of_s(n):
                dve.wait_ge(sT_hi_ready, n + 1)
                for j in range(NB):
                    last = nc.vector.tensor_tensor(sT_lo[:, j * EPB:(j + 1) * EPB, :],
                                                   sT_ps[j][:].rearrange("p (e t) -> p e t", t=P),
                                                   f32(sT_hi[:, j * EPB:(j + 1) * EPB, :]), ALU.subtract)
                last.then_inc(sT_lo_ready, 1)

            def gate_ffn(n):
                dve.wait_ge(ffn_mm, n + 1)
                wait(dve, out_ready, n)
                nc.vector.tensor_tensor(ffn[:], ffn_ps[:], mods[:, GB, n // TB, :], ALU.mult).then_inc(ffn_ready, 1)

            def step(i, has_prev, has_next, has_second, has_third):
                top2(i)
                scale_up(i)
                if has_next:
                    add_attention(i + 1)
                if has_second:
                    rest_of_qz(i + 2)
                if has_next:
                    norm_2(i + 1)
                if has_prev:
                    gate_ffn(i - 1)
                if has_third:
                    normalise_q(i + 3)
                if has_next:
                    rest_of_hT(NT + i + 1)
                rest_of_s(i)

            dve.wait_ge(ksum_ready, B)
            normalise_q(0)
            rest_of_qz(0)
            normalise_q(1)
            add_attention(0)
            rest_of_qz(1)
            norm_2(0)
            normalise_q(2)
            rest_of_hT(NT)
            for g in range(2):
                e = slice(g * E // 2, (g + 1) * E // 2)
                dve.wait_ge(wb_hi_ready, g + 1)
                nc.vector.tensor_tensor(wb_lo[:, e, :], wb_raw[:, e, :], f32(wb_hi[:, e, :]),
                                        ALU.subtract).then_inc(wb_ready, 1)
            step(0, False, True, True, True)
            with dve.Fori(1, NT - 3) as i:
                step(i, True, True, True, True)
            for i in range(NT - 3, NT):
                step(i, True, i + 1 < NT, i + 2 < NT, i + 3 < NT)
            gate_ffn(NT - 1)

        @block.tensor
        def _(pe):
            mm = nc.tensor.matmul

            def modulation(n):
                pe.wait_ge(wmod_in[n], 16)
                wait(pe, mod_row_ready, n - 1)
                for k in range(KC):
                    last = mm(m_ps[n % 2][0:B, :], silu_c[:, k, :], wmod_raw[n][:, k, :], start=(k == 0), stop=(k == KC - 1))
                last.then_inc(mod_mm, 1)

            def transpose_h(m):
                pe.wait_ge(h_ready, m + 1)
                for k in range(KC):
                    last = nc.tensor.transpose(hT_ps[:, cols(k)], h[:, cols(k)], ident[:])
                last.then_inc(h_transposed, 1)

            def project(dst, hi, lo, w_hi_of, w_lo_of, hi_ready=None, lo_ready=None):
                for k in range(KC):
                    mm(dst, hi[:, cols(k)], w_hi_of(k), start=(k == 0), stop=False)
                    mm(dst, hi[:, cols(k)], w_lo_of(k), start=False, stop=False)
                if lo_ready is not None:
                    pe.wait_ge(*lo_ready)
                for k in range(KC):
                    last = mm(dst, lo[:, cols(k)], w_hi_of(k), start=False, stop=(k == KC - 1))
                return last

            def project_h(j, dst):
                return project(dst[:], hT_hi, hT_lo, lambda k: w_hi[:, j, k, :], lambda k: w_lo[:, j, k, :])

            pe.wait_ge(silu_ready, 1)
            modulation(0)
            modulation(1)
            pe.wait_ge(const_ready, CONSTANTS)
            pe.wait_ge(ident_ready, 1)
            transpose_h(0)

            def tile(i, t, has_next):
                pe.wait_ge(hT_hi_ready, i + 1)
                pe.wait_ge(hT_lo_ready, i + 1)
                wait(pe, k_parts, i)
                if isinstance(i, int) and i == 0:
                    pe.wait_ge(w_lo_ready, 1)
                project_h(K, k_ps).then_inc(k_mm, 1)
                wait(pe, v_ready, i)
                if isinstance(i, int) and i == 0:
                    pe.wait_ge(w_lo_ready, 2)
                project_h(V, v_ps).then_inc(v_mm, 1)
                wait(pe, q_parts, i)
                if isinstance(i, int) and i == 0:
                    pe.wait_ge(w_lo_ready, 3)
                project_h(Q, q_ps).then_inc(q_mm, 1)
                if has_next:
                    transpose_h(i + 1)
                pe.wait_ge(k_ready, i + 1)
                pe.wait_ge(v_ready, i + 1)
                if t == 0:
                    wait(pe, kv_ready, i // TB)
                for j in range(KC):
                    last = mm(kv_ps[:, cols(j)], v_sb[:, cols(j)], k_sb[:, cols(j)],
                              start=(t == 0 and j == 0), stop=(t == TB - 1), skip_group_check=True)
                last.then_inc(kv_mm, 1)

            for b in range(B):
                tile(b * TB, 0, True)
                if b == 0:
                    for n in range(2, 6):
                        modulation(n)
                with pe.Fori(1, TB - 1) as t:
                    tile(b * TB + t, None, True)
                tile(b * TB + TB - 1, TB - 1, b + 1 < B)
                pe.wait_ge(k_added, (b + 1) * TB)
                wait(pe, ksum_ready, b)
                mm(ksum_ps[:], ones[:], k_acc[:], start=True, stop=True).then_inc(ksum_mm, 1)
                if b == 0:
                    pe.wait_ge(wo_in, 16)
                pe.wait_ge(kv_ready, b + 1)
                for j in range(KC):
                    n = b * KC + j
                    wait(pe, m_gated, n - 1)
                    mm(m_ps[n % 2][:], kv_sb[:, cols(j)], wo_f[:, j, :], start=True, stop=True).then_inc(m_mm, 1)

            def transpose_qz(n, bank_read):
                pe.wait_ge(qz_ready, n + 1)
                if bank_read is not None:
                    pe.wait_ge(*bank_read)
                for k in range(KC):
                    last = nc.tensor.transpose(t_ps[:, cols(k)], qz[:, cols(k)], ident[:])
                last.then_inc(qz_transposed, 1)

            def attention(n):
                b = n // TB
                pe.wait_ge(qzT_hi_ready, n + 1)
                wait(pe, x1_ready, n)
                project(attn_ps[:], qzT_hi, qzT_lo, lambda k: m_hi[:, b, k, :], lambda k: m_lo[:, b, k, :],
                        lo_ready=(qzT_lo_ready, n + 1)).then_inc(attn_mm, 1)

            def experts_up(i):
                pe.wait_ge(hT_hi_ready, NT + i + 1)
                wait(pe, logits_ready, i)
                wait(pe, s_ready, i)
                for k in range(KC):
                    mm(logit_ps[:, 0:2 * E], hT_hi[:, cols(k)], router_2[:, k, :], start=(k == 0), stop=False)
                for k in range(KC):
                    for j in range(NB):
                        mm(up_ps[j][:], hT_hi[:, cols(k)], wa_hi[:, k, cols(j, C)], start=(k == 0), stop=False)
                        mm(up_ps[j][:], hT_hi[:, cols(k)], wa_lo[:, k, cols(j, C)], start=False, stop=False)
                pe.wait_ge(hT_lo_ready, NT + i + 1)
                for k in range(KC):
                    last = mm(logit_ps[:, 0:2 * E], hT_lo[:, cols(k)], router_2[:, k, :], start=False, stop=(k == KC - 1))
                last.then_inc(logit_mm, 1)
                for k in range(KC):
                    for j in range(NB):
                        last = mm(up_ps[j][:], hT_lo[:, cols(k)], wa_hi[:, k, cols(j, C)], start=False, stop=(k == KC - 1))
                last.then_inc(up_mm, 1)

            def experts_down(n):
                pe.wait_ge(sT_hi_ready, n + 1)
                wait(pe, ffn_ready, n)
                for e in range(E):
                    mm(ffn_ps[:], sT_hi[:, e, :], wb_hi[:, e, :], start=(e == 0), stop=False)
                    mm(ffn_ps[:], sT_hi[:, e, :], wb_lo[:, e, :], start=False, stop=False)
                pe.wait_ge(sT_lo_ready, n + 1)
                for e in range(E):
                    last = mm(ffn_ps[:], sT_lo[:, e, :], wb_hi[:, e, :], start=False, stop=(e == E - 1))
                last.then_inc(ffn_mm, 1)

            def transpose_s(i):
                pe.wait_ge(s_ready, i + 1)
                wait(pe, sT_lo_ready, i)
                for e in range(E):
                    last = nc.tensor.transpose(sT_ps[e // EPB][:, cols(e % EPB)], s_sb[:, cols(e)], ident[:])
                last.then_inc(s_transposed, 1)

            def step(i, has_prev, has_next, has_second):
                experts_up(i)
                if has_second:
                    transpose_qz(i + 2, (hT_lo_ready, NT + i + 1))
                if has_next:
                    attention(i + 1)
                if has_prev:
                    experts_down(i - 1)
                if has_next:
                    if has_second:
                        pe.wait_ge(qzT_lo_ready, i + 3)
                    transpose_h(NT + i + 1)
                transpose_s(i)

            transpose_qz(0, None)
            attention(0)
            transpose_qz(1, (qzT_lo_ready, 1))
            pe.wait_ge(qzT_lo_ready, 2)
            transpose_h(NT)
            pe.wait_ge(router_ready, 1)
            step(0, False, True, True)
            pe.wait_ge(wb_ready, 2)
            with pe.Fori(1, NT - 3) as i:
                step(i, True, True, True)
            for i in range(NT - 3, NT):
                step(i, True, i + 1 < NT, i + 2 < NT)
            experts_down(NT - 1)


def kernel(L0_attn_x, L0_attn_cos, L0_attn_sin, L0_attn_Wq, L0_attn_Wk, L0_attn_Wv, L0_attn_Wo,
           L0_ffn_router_w, L0_ffn_Wa, L0_ffn_Wb, L0_c, L0_wmod):
    import concourse.bacc as bacc
    import numpy as np
    from concourse.bass_utils import run_bass_kernel_spmd

    def dense(a):
        return np.ascontiguousarray(a)

    x = np.asarray(L0_attn_x)
    c = np.asarray(L0_c)
    experts, features, rank = L0_ffn_Wa.shape
    chunks = features // P
    arrays = {
        "x": dense(x.reshape(-1, features)),
        "c_cols": dense(c.T.reshape(chunks, P, -1).transpose(1, 0, 2)),
        "wq": dense(np.asarray(L0_attn_Wq).T),
        "wk": dense(np.asarray(L0_attn_Wk).T),
        "wv": dense(np.asarray(L0_attn_Wv).T),
        "wo": dense(np.asarray(L0_attn_Wo).T),
        "router": dense(np.asarray(L0_ffn_router_w).reshape(chunks, P, -1).transpose(1, 0, 2)),
        "wa": dense(np.asarray(L0_ffn_Wa).transpose(1, 0, 2).reshape(features, experts * rank)),
        "wb": dense(L0_ffn_Wb),
        "wmod": dense(L0_wmod),
    }
    nc = bacc.Bacc("TRN2", target_bir_lowering=False, num_devices=1)
    args = [nc.dram_tensor(name, a.shape, mybir.dt.from_np(a.dtype), kind="ExternalInput").ap()
            for name, a in arrays.items()]
    mod_rows = nc.dram_tensor("mod_rows", (6, c.shape[0], features), F32).ap()
    out = nc.dram_tensor("out", arrays["x"].shape, F32, kind="ExternalOutput").ap()
    adaln_block(nc, *args, mod_rows, out)
    result = run_bass_kernel_spmd(nc, [arrays], core_ids=[0])
    return result.results[0]["out"].reshape(x.shape)
```

```python
from contextlib import ExitStack

import concourse.bass as bass
from concourse import mybir

ALU = mybir.AluOpType
ACT = mybir.ActivationFunctionType
AX = mybir.AxisListType
F32 = mybir.dt.float32
F32R = mybir.dt.float32r
U32 = mybir.dt.uint32

P = 128
LN_EPS = 1e-5
DEN_EPS = 1e-6
NORM_FLOOR = 1e-12
GATE_FLOOR = 0.25
KB = 1024
CA, SA, SB, CB, GA, GB = range(6)
IN_WMOD = [1, 0, 3, 4, 2, 5]
Q, K, V = range(3)


def adaln_block(nc, x, c_cols, wq, wk, wv, wo, router, wa, wb, wmod, out):
    TOK, C = x.shape
    B = c_cols.shape[2]
    E, R, _ = wb.shape
    KC = C // P
    NT = TOK // P
    TB = NT // B
    DH = 32
    H = C // DH
    NB = E * R // C
    EPB = E // NB
    assert C == 512 and R == P and E == 8 and NT * P == TOK and TB * B == NT and TB == KC * NB == 8 and B == 2

    x_t = x.rearrange("(n p) c -> p n c", p=P)
    out_t = out.rearrange("(n p) c -> p n c", p=P)

    def chunked(w):
        return w.rearrange("(k p) n -> p k n", p=P)

    BASE = 16512
    ROW = C * 4
    WQKV_AT = BASE
    WO_AT = WQKV_AT + 2 * 3 * KC * ROW
    XQ_AT = WO_AT + KC * ROW
    U_AT = XQ_AT + NT * ROW
    WA_AT = U_AT + 2 * B * KC * ROW
    MODS_AT = WA_AT + 2 * KC * NB * ROW
    STAGE_AT = MODS_AT + 6 * B * ROW
    SMALL_AT = STAGE_AT + 13 * ROW

    def at(name, shape, dt, offset):
        return nc.alloc_sbuf_tensor_at(name, shape, dt, offset=offset)

    w_hi = at("w_hi", [P, 3, KC, C], F32R, WQKV_AT)
    w_lo = at("w_lo", [P, 3, KC, C], F32R, WQKV_AT + 3 * KC * ROW)
    wb_hi = at("wb_hi", [P, E, C], F32R, WQKV_AT)
    wb_lo = at("wb_lo", [P, E, C], F32R, WQKV_AT + E * ROW)
    wo_f = at("wo_f", [P, KC, C], F32, WO_AT)
    sT_hi = at("sT_hi", [P, E, P], F32R, WO_AT)
    sT_lo = at("sT_lo", [P, E, P], F32R, WO_AT + 2 * ROW)
    xq = at("xq", [P, NT, C], F32, XQ_AT)
    m_hi = at("m_hi", [P, B, KC, C], F32R, U_AT)
    m_lo = at("m_lo", [P, B, KC, C], F32R, U_AT + B * KC * ROW)
    wa_hi = at("wa_hi", [P, KC, E * R], F32R, WA_AT)
    wa_lo = at("wa_lo", [P, KC, E * R], F32R, WA_AT + KC * NB * ROW)
    wmod_raw = at("wmod_raw", [P, 6, KC, C], F32, U_AT)
    raw = at("w_raw", [P, 3, KC, C], F32, WQKV_AT + 3 * KC * ROW)
    wb_raw = at("wb_raw", [P, E, C], F32, WQKV_AT + E * ROW)
    wa_raw = at("wa_raw", [P, KC, E * R], F32, WA_AT + KC * NB * ROW)
    mods = at("mods", [P, 6, B, C], F32, MODS_AT)

    def stage(name, n, dt=F32, rows=1, shape=None):
        return at(name, shape or [P, rows * C], dt, STAGE_AT + n * ROW)

    h = stage("h", 0)
    hT_hi = stage("hT_hi", 1, F32R)
    hT_lo = stage("hT_lo", 2, F32R)
    exp_k, relu_k = stage("exp_k", 3), stage("relu_k", 4)
    exp_q, relu_q = stage("exp_q", 5), stage("relu_q", 6)
    k_sb, v_sb = stage("k_sb", 7), stage("v_sb", 8)
    k_acc = stage("k_acc", 9)
    kv_sb = stage("kv_sb", 10)
    mod_acc = [stage("mod_acc0", 11), stage("mod_acc1", 12)]
    silu_wide = at("silu_wide", [P, KC, P], F32, STAGE_AT + 9 * ROW)
    gate_sign = at("gate_sign", [P, C], F32, STAGE_AT + 10 * ROW)
    qzT_hi, qzT_lo = stage("qzT_hi", 3, F32R), stage("qzT_lo", 4, F32R)
    s_sb = stage("s_sb", 7, rows=NB)
    q_ksum = at("q_ksum", [P, C], F32, MODS_AT + (SA * B + 0) * ROW)
    qz = at("qz", [P, C], F32, MODS_AT + (SA * B + 1) * ROW)
    square = at("square", [P, C], F32, MODS_AT + (GA * B + 0) * ROW)
    ffn = at("ffn", [P, C], F32, MODS_AT + (GA * B + 1) * ROW)

    small_end = [SMALL_AT]

    def small(name, shape, dt=F32):
        n = 1
        for d in shape[1:]:
            n *= d
        t = at(name, shape, dt, small_end[0])
        small_end[0] += -(-n * 4 // 32) * 32
        return t

    ident = small("ident", [P, P])
    ones = small("ones", [P, P])
    head_mask = small("head_mask", [P, P])
    router_raw = small("router_raw", [P, KC, E])
    router_2 = small("router_2", [P, KC, 2 * E], F32R)
    c_sb = small("c_sb", [P, KC, B])
    exp_c = small("exp_c", [P, KC, B])
    silu_c = small("silu_c", [P, KC, B])
    minus_half = small("minus_half", [P, 1])
    mod_bias = small("mod_bias", [P, 6])
    logits_T = small("logits_T", [2 * E, P])
    expert_no = small("expert_no", [P, E])
    bn6 = small("bn6", [P, 6])
    mean_var = small("mean_var", [P, 2])
    var_eps = small("var_eps", [P, 1])
    rstd = small("rstd", [P, 1])
    den = small("den", [P, H])
    den_eps = small("den_eps", [P, H])
    z = small("z", [P, H])
    sq_sum = small("sq_sum", [P, 1])
    sq_floor = small("sq_floor", [P, 1])
    inv_norm = small("inv_norm", [P, 1])
    logit_lo = small("logit_lo", [P, E])
    logits = small("logits", [P, E])
    top = small("top", [P, 8])
    top_at = small("top_at", [P, 8], U32)
    top_at_f = small("top_at_f", [P, 2])
    gap = small("gap", [P, 1])
    ratio = small("ratio", [P, 1])
    ratio_1 = small("ratio_1", [P, 1])
    weight = small("weight", [P, 2])
    combine_0 = small("combine_0", [P, E])
    combine_1 = small("combine_1", [P, E])
    combine = small("combine", [P, E])

    with ExitStack() as ctx:
        banks = [ctx.enter_context(nc.psum_tensor(f"bank{n}", [P, C], F32)) for n in range(8)]
        k_ps, v_ps, q_ps, hT_ps, kv_ps, ksum_ps = banks[:6]
        mod_ps = banks[6:8]
        direct_ps = {CA: ksum_ps, SA: kv_ps}
        m_ps = [banks[6:8] + [q_ps, kv_ps], banks[6:8] + [k_ps, v_ps]]
        up_ps = banks[0:2]
        attn_ps, t_ps, ffn_ps, logit_ps = banks[2:6]
        sT_ps = banks[6:8]

        def sem(name):
            return ctx.enter_context(nc.semaphore(name))

        c_in, wo_in, router_in, wa_in, wb_in = (sem(s) for s in ("c_in", "wo_in", "router_in", "wa_in", "wb_in"))
        ca_in, sa_in = ([sem(f"{row}_in{g}") for g in range(2)] for row in ("ca", "sa"))
        sb_in, wmod_in = sem("sb_in"), sem("wmod_in")
        w_in = {j: sem(f"w_in{j}") for j in (Q, K, V)}
        x_in = [sem(f"x_in{n}") for n in range(4)]
        x_again = sem("x_again")
        out_done = sem("out_done")
        const_step, const_ready, ident_ready = sem("const_step"), sem("const_ready"), sem("ident_ready")
        c_exp, silu_step, silu_ready, silu_wide_ready = (sem(s) for s in ("c_exp", "silu_step", "silu_ready", "silu_wide_ready"))
        mod_step, mod_acc_ready, mod_mm, mod_ready = (sem(s) for s in ("mod_step", "mod_acc_ready", "mod_mm", "mod_ready"))
        gate_step, gates_ready, wo_gated = sem("gate_step"), sem("gates_ready"), sem("wo_gated")
        w_hi_ready, w_lo_ready = sem("w_hi_ready"), sem("w_lo_ready")
        router_hi_ready, router_ready = sem("router_hi_ready"), sem("router_ready")
        wa_hi_ready, wa_ready = sem("wa_hi_ready"), sem("wa_ready")
        wb_hi_ready, wb_ready = sem("wb_hi_ready"), sem("wb_ready")
        bn_ready, stats_ready, var_ready, rstd_ready = (sem(s) for s in ("bn_ready", "stats_ready", "var_ready", "rstd_ready"))
        scaled_ready, h_ready = sem("scaled_ready"), sem("h_ready")
        h_transposed, hT_hi_ready, hT_lo_ready = (sem(s) for s in ("h_transposed", "hT_hi_ready", "hT_lo_ready"))
        k_mm, v_mm, q_mm, kv_mm = (sem(s) for s in ("k_mm", "v_mm", "q_mm", "kv_mm"))
        k_parts, q_parts = sem("k_parts"), sem("q_parts")
        k_ready, v_ready, q_ready, k_added = (sem(s) for s in ("k_ready", "v_ready", "q_ready", "k_added"))
        ksum_mm, ksum_ready, kv_ready = sem("ksum_mm"), sem("ksum_ready"), sem("kv_ready")
        m_mm, m_hi_ready, m_ready = sem("m_mm"), sem("m_hi_ready"), sem("m_ready")
        q_ksum_ready, den_step, qz_ready, qz_transposed = (sem(s) for s in ("q_ksum_ready", "den_step", "qz_ready", "qz_transposed"))
        qzT_hi_ready, qzT_lo_ready = sem("qzT_hi_ready"), sem("qzT_lo_ready")
        attn_mm, x1_ready = sem("attn_mm"), sem("x1_ready")
        sq_ready, sq_floored, norm_ready = sem("sq_ready"), sem("sq_floored"), sem("norm_ready")
        logit_T_mm, logits_T_ready = sem("logit_T_mm"), sem("logits_T_ready")
        logit_mm, logits_ready, top2_step, ratio_ready = (sem(s) for s in ("logit_mm", "logits_ready", "top2_step", "ratio_ready"))
        up_mm, s_ready, s_transposed = sem("up_mm"), sem("s_ready"), sem("s_transposed")
        sT_hi_ready, sT_lo_ready = sem("sT_hi_ready"), sem("sT_lo_ready")
        ffn_mm, ffn_ready, out_ready, last_out_ready = (sem(s) for s in ("ffn_mm", "ffn_ready", "out_ready", "last_out_ready"))

        sp_passed, pool_passed, dve_passed, act_passed, pe_passed = (
            sem(s) for s in ("sp_passed", "pool_passed", "dve_passed", "act_passed", "pe_passed"))

        def wait(eng, s, value):
            if not (isinstance(value, int) and value <= 0):
                eng.wait_ge(s, value)

        def wait_apart(eng, passed, s, value):
            wait(eng, s, value)
            if not isinstance(value, int):
                eng.sem_inc(passed, 1)

        def cols(j, width=P):
            return slice(j * width, (j + 1) * width)

        def f32(t):
            return t.bitcast(F32)

        LOGITS = 2 * P
        CONSTANTS = 6 + P // DH + E
        TOP2 = 10

        block = ctx.enter_context(nc.Block())

        @block.sync
        def _(sp):
            def load_wmod(n):
                j = IN_WMOD[n]
                return sp.dma_start(wmod_raw[:, n, :, :], chunked(wmod[:, cols(j, C)]))

            def load_wo(b):
                return sp.dma_start(wo_f[:], chunked(wo)).then_inc(wo_in, 16)

            sp.dma_start(c_sb[:], c_cols).then_inc(c_in, 16)
            for n, arrived in ((CA, ca_in), (SA, sa_in)):
                for g in range(2):
                    k = slice(g * KC // 2, (g + 1) * KC // 2)
                    sp.dma_start(wmod_raw[:, n, k, :], chunked(wmod[:, cols(IN_WMOD[n], C)])[:, k, :]).then_inc(arrived[g], 16)
            sp.dma_start(xq[:, 0, :], x_t[:, 0, :]).then_inc(x_in[0], 16)
            for j, w in ((K, wk), (V, wv), (Q, wq)):
                sp.dma_start(raw[:, j, :, :], chunked(w)).then_inc(w_in[j], 16)
                if j == V:
                    sp.dma_start(xq[:, 1, :], x_t[:, 1, :]).then_inc(x_in[1], 16)
            load_wmod(SB).then_inc(sb_in, 16)
            sp.dma_start(xq[:, 2:TB, :], x_t[:, 2:TB, :]).then_inc(x_in[2], 16)
            for n in (CB, GA, GB):
                load_wmod(n).then_inc(wmod_in, 16)
            load_wo(0)
            sp.dma_start(router_raw[:], router).then_inc(router_in, 16)
            sp.dma_start(wa_raw[:], chunked(wa)).then_inc(wa_in, 16)
            sp.dma_start(xq[:, TB:NT, :], x_t[:, TB:NT, :]).then_inc(x_in[3], 16)
            sp.wait_ge(m_mm, KC)
            load_wo(1)
            def reload_x(n):
                sp.wait_ge(qz_ready, n + 1)
                sp.dma_start(xq[:, n, :], x_t[:, n, :]).then_inc(x_again, 16)
                wait_apart(sp, sp_passed, x_again, 16 * (n + 1))

            def store(n):
                sp.wait_ge(out_ready, n + 1)
                sp.dma_start(out_t[:, n, :], xq[:, n, :]).then_inc(out_done, 16)

            reload_x(0)
            sp.wait_ge(q_mm, NT)
            sp.dma_start(wb_raw[:], wb.rearrange("e r c -> r e c")).then_inc(wb_in, 16)
            LAG = 4
            with sp.Fori(1, LAG) as n:
                reload_x(n)
            with sp.Fori(LAG, NT) as n:
                reload_x(n)
                store(n - LAG)
            with sp.Fori(NT - LAG, NT - 1) as n:
                store(n)
            sp.wait_ge(last_out_ready, 1)
            sp.dma_start(out_t[:, NT - 1, :], xq[:, NT - 1, :]).then_inc(out_done, 16)
            sp.wait_ge(out_done, 16 * NT)

        @block.gpsimd
        def _(pool):
            nc.gpsimd.memset(ident[:], 1.0).then_inc(const_step, 1)
            pool.wait_ge(const_step, 1)
            nc.gpsimd.affine_select(out=ident[:], in_=ident[:], compare_op=ALU.is_equal, fill=0.0, base=0,
                                    pattern=[[-1, P]], channel_multiplier=1).then_inc(ident_ready, 1)
            pool.wait_ge(ident_ready, 1)
            pool.wait_ge(const_ready, CONSTANTS)

            def inverse_std(m):
                pool.wait_ge(stats_ready, m + 1)
                wait_apart(pool, pool_passed, h_ready, m)
                nc.gpsimd.tensor_scalar(var_eps[:], mean_var[:, 1:2], LN_EPS, None, ALU.add).then_inc(var_ready, 1)
                pool.wait_ge(var_ready, m + 1)
                nc.gpsimd.tensor_tensor(rstd[:], var_eps[:], minus_half[:], ALU.pow).then_inc(rstd_ready, 1)

            inverse_std(0)

            def add_k(i, first):
                pool.wait_ge(k_ready, i + 1)
                if first:
                    wait(pool, ksum_mm, i // TB)
                    nc.gpsimd.tensor_copy(k_acc[:], k_sb[:]).then_inc(k_added, 1)
                else:
                    pool.wait_ge(k_added, i)
                    nc.gpsimd.tensor_tensor(k_acc[:], k_acc[:], k_sb[:], ALU.add).then_inc(k_added, 1)

            def split_wa(t):
                here = cols(t, C) if isinstance(t, int) else bass.ts(t, C)
                hi, lo, src = (w[:].rearrange("p k n -> p (k n)")[:, here] for w in (wa_hi, wa_lo, wa_raw))
                nc.gpsimd.tensor_copy(hi, src).then_inc(wa_hi_ready, 1)
                wait_apart(pool, pool_passed, wa_hi_ready, t + 1)
                nc.gpsimd.tensor_tensor(lo, src, f32(hi), ALU.subtract).then_inc(wa_ready, 1)

            def gate_wo(b):
                pool.wait_ge(wo_in, 16 * (b + 1))
                pool.wait_ge(gates_ready, 2)
                nc.gpsimd.tensor_tensor(wo_f[:], wo_f[:], mods[:, GA, b, :].unsqueeze(1).broadcast_to((P, KC, C)),
                                        ALU.mult).then_inc(wo_gated, 1)

            for b in range(B):
                i = b * TB
                inverse_std(i + 1)
                add_k(i, True)
                if b == 1:
                    pool.wait_ge(wa_in, 16)
                    pool.wait_ge(mod_acc_ready, 6 * B - 2)
                    split_wa(0)
                with pool.Fori(1, TB - 2) as t:
                    inverse_std(b * TB + t + 1)
                    add_k(b * TB + t, False)
                    if b == 1:
                        split_wa(t)
                for t in (TB - 2, TB - 1):
                    i = b * TB + t
                    if i + 1 < NT:
                        inverse_std(i + 1)
                    if t == TB - 2:
                        gate_wo(b)
                    add_k(i, False)
                    if b == 1:
                        split_wa(t)

            def inverse_norm(n):
                pool.wait_ge(sq_ready, n + 1)
                wait_apart(pool, pool_passed, logits_ready, n)
                nc.gpsimd.tensor_scalar(sq_floor[:], sq_sum[:], NORM_FLOOR * NORM_FLOOR, None, ALU.max).then_inc(sq_floored, 1)
                pool.wait_ge(sq_floored, n + 1)
                nc.gpsimd.tensor_tensor(inv_norm[:], sq_floor[:], minus_half[:], ALU.pow).then_inc(norm_ready, 1)

            def add_ffn(n):
                pool.wait_ge(ffn_ready, n + 1)
                nc.gpsimd.tensor_tensor(xq[:, n, :], xq[:, n, :], ffn[:], ALU.add).then_inc(out_ready, 1)

            def step(i, has_prev, has_next):
                if has_next:
                    inverse_std(NT + i + 1)
                    inverse_norm(i + 1)
                if has_prev:
                    add_ffn(i - 1)

            inverse_std(NT)
            inverse_norm(0)
            step(0, False, True)
            with pool.Fori(1, NT - 3) as i:
                step(i, True, True)
            for i in range(NT - 3, NT):
                step(i, True, i + 1 < NT)

        @block.scalar
        def _(act):
            act.wait_ge(c_in, 16)
            nc.scalar.activation(exp_c[:], c_sb[:], ACT.Exp, scale=-1.0).then_inc(c_exp, 1)

            def split_w(j):
                act.wait_ge(w_in[j], 16)
                nc.scalar.activation(w_hi[:, j, :, :], raw[:, j, :, :], ACT.Copy).then_inc(w_hi_ready, 1)

            def spread_mod(u, bank, n, b):
                wait_apart(act, act_passed, mod_mm, u + 1)
                nc.scalar.activation(mods[:, n, b, :], bank[:], ACT.Identity,
                                     bias=mod_bias[:, bass.ds(n, 1)]).then_inc(mod_ready, 1)

            def split_hT(m, last_read=None):
                act.wait_ge(h_transposed, m + 1)
                if last_read is not None:
                    act.wait_ge(*last_read)
                nc.scalar.activation(hT_hi[:], hT_ps[:], ACT.Copy).then_inc(hT_hi_ready, 1)

            act.wait_ge(const_ready, CONSTANTS)
            spread_mod(0, mod_ps[0], CA, 0)
            spread_mod(1, mod_ps[1], SA, 0)
            split_w(K)
            split_hT(0)
            split_w(V)
            spread_mod(2, direct_ps[CA], CA, 1)
            spread_mod(3, direct_ps[SA], SA, 1)
            split_w(Q)

            def phi_parts_k(i):
                act.wait_ge(k_mm, i + 1)
                wait(act, k_ready, i)
                nc.scalar.activation(exp_k[:], k_ps[:], ACT.Exp)
                nc.scalar.activation(relu_k[:], k_ps[:], ACT.Relu).then_inc(k_parts, 1)

            def copy_v(i):
                act.wait_ge(v_mm, i + 1)
                wait(act, kv_mm, i)
                nc.scalar.activation(v_sb[:], v_ps[:], ACT.Copy).then_inc(v_ready, 1)

            def phi_parts_q(i):
                act.wait_ge(q_mm, i + 1)
                wait(act, q_ready, i)
                nc.scalar.activation(exp_q[:], q_ps[:], ACT.Exp)
                nc.scalar.activation(relu_q[:], q_ps[:], ACT.Relu).then_inc(q_parts, 1)

            def tile(i, row=None, k_done=False):
                if not k_done:
                    phi_parts_k(i)
                if row is not None:
                    for b in range(B):
                        spread_mod(B * row + b, mod_ps[b], row, b)
                copy_v(i)
                split_hT(i + 1, (q_mm, i + 1))
                phi_parts_q(i)

            def sum_k_out(b):
                act.wait_ge(ksum_mm, b + 1)
                act.wait_ge(h_ready, (b + 1) * TB)
                nc.scalar.activation(mods[:, CA, b, :], ksum_ps[:], ACT.Copy).then_inc(ksum_ready, 1)

            def split_m(b):
                for j in range(KC):
                    act.wait_ge(m_mm, b * KC + j + 1)
                    nc.scalar.activation(m_hi[:, b, j, :], m_ps[b][j][:], ACT.Copy).then_inc(m_hi_ready, 1)

            tile(0)
            tile(1)
            with act.Fori(2, 6) as t:
                tile(t, t)
            for i in (TB - 2, TB - 1):
                tile(i)
            sum_k_out(0)
            phi_parts_k(TB)
            split_m(0)
            tile(TB, k_done=True)
            with act.Fori(TB + 1, NT - 1) as i:
                tile(i)

            def split_qz(n):
                act.wait_ge(qz_transposed, n + 1)
                wait(act, attn_mm, n)
                nc.scalar.activation(qzT_hi[:], t_ps[:], ACT.Copy).then_inc(qzT_hi_ready, 1)

            def square_sum(n):
                act.wait_ge(h_ready, NT + n + 1)
                wait(act, norm_ready, n)
                nc.scalar.activation(square[:], h[:], ACT.Square, accum_out=sq_sum[:]).then_inc(sq_ready, 1)

            def weights(i):
                act.wait_ge(logit_T_mm, i + 1)
                nc.scalar.activation(logits_T[:], logit_ps[0:2 * E, 0:P], ACT.Copy).then_inc(logits_T_ready, 1)
                act.wait_ge(top2_step, TOP2 * i + 4)
                nc.scalar.activation(ratio[:], gap[:], ACT.Exp).then_inc(ratio_ready, 1)

            def split_sT(i):
                for j in range(NB):
                    act.wait_ge(s_transposed, NB * i + j + 1)
                    nc.scalar.activation(sT_hi[:, j * EPB:(j + 1) * EPB, :], sT_ps[j][:], ACT.Copy).then_inc(sT_hi_ready, 1)

            def first_step():
                weights(0)
                square_sum(1)
                split_qz(2)
                split_sT(0)
                split_hT(NT + 1)

            def step(i, has_next, has_second):
                weights(i)
                if has_second:
                    split_qz(i + 2)
                if has_next:
                    square_sum(i + 1)
                    split_hT(NT + i + 1)
                split_sT(i)

            phi_parts_k(NT - 1)
            copy_v(NT - 1)
            act.wait_ge(k_ready, NT)
            split_qz(0)
            phi_parts_q(NT - 1)
            sum_k_out(1)
            split_qz(1)
            split_m(1)
            square_sum(0)
            split_hT(NT)
            first_step()
            act.wait_ge(wb_in, 16)
            for g in range(2):
                e = slice(g * E // 2, (g + 1) * E // 2)
                nc.scalar.activation(wb_hi[:, e, :], wb_raw[:, e, :], ACT.Copy).then_inc(wb_hi_ready, 1)
            with act.Fori(1, NT - 3) as i:
                step(i, True, True)
            for i in range(NT - 3, NT):
                step(i, i + 1 < NT, i + 2 < NT)

        @block.vector
        def _(dve):
            nc.vector.memset(head_mask[:], 0.0).then_inc(const_ready, 1)
            dve.wait_ge(const_ready, 1)
            for j in range(P // DH):
                nc.vector.memset(head_mask[cols(j, DH), cols(j, DH)], 1.0).then_inc(const_ready, 1)
            nc.vector.memset(ones[:], 1.0).then_inc(const_ready, 1)
            nc.vector.memset(minus_half[:], -0.5).then_inc(const_ready, 1)
            for e in range(E):
                nc.vector.memset(expert_no[:, e:e + 1], float(e)).then_inc(const_ready, 1)
            nc.vector.memset(mod_bias[:], 0.0).then_inc(const_ready, 1)
            dve.wait_ge(const_ready, CONSTANTS - 2)
            for n in (CA, CB):
                nc.vector.memset(mod_bias[:, n:n + 1], 1.0).then_inc(const_ready, 1)
            dve.wait_ge(const_ready, CONSTANTS)
            dve.wait_ge(c_exp, 1)
            nc.vector.tensor_scalar(exp_c[:], exp_c[:], 1.0, None, ALU.add).then_inc(silu_step, 1)
            dve.wait_ge(silu_step, 1)
            nc.vector.reciprocal(exp_c[:], exp_c[:]).then_inc(silu_step, 1)
            dve.wait_ge(silu_step, 2)
            nc.vector.tensor_tensor(silu_c[:], exp_c[:], c_sb[:], ALU.mult).then_inc(silu_ready, 1)
            dve.wait_ge(silu_ready, 1)
            nc.vector.tensor_tensor(silu_wide[:], ones[:].unsqueeze(1).broadcast_to((P, KC, P)),
                                    silu_c[:, :, 1].unsqueeze(2).broadcast_to((P, KC, P)), ALU.mult).then_inc(silu_wide_ready, 1)

            def mod_sum(d, n, b, arrived=None):
                acc = mod_acc[b if arrived is None else d]
                if arrived is not None:
                    dve.wait_ge(arrived[0], 16)
                else:
                    dve.wait_ge(mod_mm, d + 1)
                nc.vector.tensor_scalar(acc[:], wmod_raw[:, n, 0, :], silu_c[:, 0, b:b + 1], None,
                                        ALU.mult).then_inc(mod_step, 1)
                for k in range(1, KC):
                    dve.wait_ge(mod_step, (KC - 1) * d + k)
                    if arrived is not None and k == KC // 2:
                        dve.wait_ge(arrived[1], 16)
                    last = nc.vector.scalar_tensor_tensor(out=acc[:], in0=wmod_raw[:, n, k, :], scalar=silu_c[:, k, b:b + 1],
                                                          in1=acc[:], op0=ALU.mult, op1=ALU.add)
                    last.then_inc(mod_step if k < KC - 1 else mod_acc_ready, 1)

            def floor_gate(g, n, b):
                gate = mods[:, n, b, :]
                nc.vector.tensor_scalar(gate_sign[:], gate, 0.0, 2.0, ALU.is_ge, ALU.mult).then_inc(gate_step, 1)
                dve.wait_ge(gate_step, 3 * g + 1)
                nc.vector.tensor_scalar(gate_sign[:], gate_sign[:], -1.0, None, ALU.add).then_inc(gate_step, 1)
                dve.wait_ge(gate_step, 3 * g + 2)
                nc.vector.tensor_tensor(gate, gate, gate_sign[:], ALU.mult).then_inc(gate_step, 1)
                dve.wait_ge(gate_step, 3 * g + 3)
                nc.vector.scalar_tensor_tensor(out=gate, in0=gate, scalar=GATE_FLOOR, in1=gate_sign[:],
                                               op0=ALU.max, op1=ALU.mult).then_inc(gates_ready, 1)
                dve.wait_ge(gates_ready, g + 1)

            def statistics(m, src):
                nc.vector.bn_stats(out=bn6[:], in_=src).then_inc(bn_ready, 1)
                dve.wait_ge(bn_ready, m + 1)
                wait_apart(dve, dve_passed, rstd_ready, m)
                nc.vector.bn_aggr(out=mean_var[:], in_=bn6[:]).then_inc(stats_ready, 1)
                dve.wait_ge(stats_ready, m + 1)

            def modulate(m, src, scale, shift):
                wait(dve, h_transposed, m)
                nc.vector.scalar_tensor_tensor(out=h[:], in0=src, scalar=mean_var[:, 0:1], in1=scale,
                                               op0=ALU.subtract, op1=ALU.mult).then_inc(scaled_ready, 1)
                dve.wait_ge(scaled_ready, m + 1)
                dve.wait_ge(rstd_ready, m + 1)
                nc.vector.scalar_tensor_tensor(out=h[:], in0=h[:], scalar=rstd[:, 0:1], in1=shift,
                                               op0=ALU.mult, op1=ALU.add).then_inc(h_ready, 1)

            def rest_of_hT(m):
                dve.wait_ge(hT_hi_ready, m + 1)
                nc.vector.tensor_tensor(hT_lo[:], hT_ps[:], f32(hT_hi[:]), ALU.subtract).then_inc(hT_lo_ready, 1)

            def rest_of_w(j, n):
                dve.wait_ge(w_hi_ready, n + 1)
                nc.vector.tensor_tensor(w_lo[:, j, :, :], raw[:, j, :, :], f32(w_hi[:, j, :, :]),
                                        ALU.subtract).then_inc(w_lo_ready, 1)

            mod_sum(0, CA, 0, ca_in)
            mod_sum(1, SA, 0, sa_in)
            dve.wait_ge(x_in[0], 16)
            statistics(0, xq[:, 0, :])
            dve.wait_ge(mod_ready, B)
            modulate(0, xq[:, 0, :], mods[:, CA, 0, :], mods[:, SA, 0, :])
            rest_of_hT(0)
            rest_of_w(K, 0)
            rest_of_w(V, 1)
            dve.wait_ge(x_in[1], 16)
            statistics(1, xq[:, 1, :])
            rest_of_w(Q, 2)
            modulate(1, xq[:, 1, :], mods[:, CA, 0, :], mods[:, SA, 0, :])

            def next_norm(i, b):
                statistics(i, xq[:, i, :])
                modulate(i, xq[:, i, :], mods[:, CA, b, :], mods[:, SA, b, :])

            def phi_k(i):
                dve.wait_ge(k_parts, i + 1)
                wait(dve, k_added, i)
                wait(dve, kv_mm, i)
                nc.vector.scalar_tensor_tensor(out=k_sb[:], in0=exp_k[:], scalar=1.0, in1=relu_k[:],
                                               op0=ALU.min, op1=ALU.add).then_inc(k_ready, 1)

            def phi_q(i):
                dve.wait_ge(q_parts, i + 1)
                nc.vector.scalar_tensor_tensor(out=xq[:, i, :], in0=exp_q[:], scalar=1.0, in1=relu_q[:],
                                               op0=ALU.min, op1=ALU.add).then_inc(q_ready, 1)

            def tile(i, b, d=None, row=None, gates=None):
                next_norm(i + 1, b)
                if row is not None:
                    mod_sum(d, row, 0)
                if gates is not None:
                    dve.wait_ge(mod_ready, B * (gates + GA + 1))
                    floor_gate(B * gates, gates + GA, 0)
                phi_k(i)
                if row is not None:
                    mod_sum(d + 1, row, 1)
                if gates is not None:
                    floor_gate(B * gates + 1, gates + GA, 1)
                rest_of_hT(i + 1)
                phi_q(i)

            def mask_kv(b):
                dve.wait_ge(kv_mm, (b + 1) * TB)
                wait(dve, m_mm, b * KC)
                nc.vector.tensor_tensor(kv_sb[:].rearrange("p (j e) -> p j e", e=P),
                                        kv_ps[:].rearrange("p (j e) -> p j e", e=P),
                                        head_mask[:].unsqueeze(1).broadcast_to((P, KC, P)),
                                        ALU.mult).then_inc(kv_ready, 1)

            def rest_of_m(b):
                for j in range(KC):
                    dve.wait_ge(m_hi_ready, b * KC + j + 1)
                    nc.vector.tensor_tensor(m_lo[:, b, j, :], m_ps[b][j][:], f32(m_hi[:, b, j, :]),
                                            ALU.subtract).then_inc(m_ready, 1)

            phi_k(0)
            rest_of_hT(1)
            phi_q(0)
            dve.wait_ge(x_in[2], 16)
            dve.wait_ge(sb_in, 16)
            tile(1, 0, B, SB)
            dve.wait_ge(wmod_in, 16 * 3)
            with dve.Fori(2, 5) as t:
                tile(t, 0, B * t, t + 1)
            for g in range(2):
                tile(TB - 3 + g, 0, gates=g)
            dve.wait_ge(router_in, 16)
            nc.vector.tensor_copy(router_2[:, :, 0:E], router_raw[:]).then_inc(router_hi_ready, 1)
            dve.wait_ge(router_hi_ready, 1)
            nc.vector.tensor_tensor(router_2[:, :, E:2 * E], router_raw[:], f32(router_2[:, :, 0:E]),
                                    ALU.subtract).then_inc(router_ready, 1)
            dve.wait_ge(x_in[3], 16)
            tile(TB - 1, 1)
            mask_kv(0)
            next_norm(TB + 1, 1)
            rest_of_m(0)
            phi_k(TB)
            rest_of_hT(TB + 1)
            phi_q(TB)
            with dve.Fori(TB + 1, NT - 1) as i:
                tile(i, 1)

            def normalise_q(n):
                ksum = mods[:, CA, n // TB, :]
                wait(dve, q_ksum_ready, n)
                nc.vector.tensor_tensor(q_ksum[:], xq[:, n, :], ksum, ALU.mult).then_inc(q_ksum_ready, 1)
                dve.wait_ge(q_ksum_ready, n + 1)
                nc.vector.tensor_reduce(den[:], q_ksum[:].rearrange("p (h d) -> p h d", d=DH), AX.X,
                                        ALU.add).then_inc(den_step, 1)
                dve.wait_ge(den_step, 3 * n + 1)
                nc.vector.tensor_scalar(den_eps[:], den[:], DEN_EPS, None, ALU.add).then_inc(den_step, 1)
                dve.wait_ge(den_step, 3 * n + 2)
                nc.vector.reciprocal(z[:], den_eps[:]).then_inc(den_step, 1)
                dve.wait_ge(den_step, 3 * n + 3)
                wait(dve, qz_transposed, n)
                nc.vector.tensor_tensor(qz[:].rearrange("p (h d) -> p h d", d=DH),
                                        xq[:, n, :].rearrange("p (h d) -> p h d", d=DH),
                                        z[:].unsqueeze(2).broadcast_to((P, H, DH)), ALU.mult).then_inc(qz_ready, 1)

            def rest_of_qz(n):
                dve.wait_ge(qzT_hi_ready, n + 1)
                nc.vector.tensor_tensor(qzT_lo[:], t_ps[:], f32(qzT_hi[:]), ALU.subtract).then_inc(qzT_lo_ready, 1)

            def add_attention(n):
                dve.wait_ge(attn_mm, n + 1)
                dve.wait_ge(x_again, 16 * (n + 1))
                nc.vector.tensor_tensor(xq[:, n, :], xq[:, n, :], attn_ps[:], ALU.add).then_inc(x1_ready, 1)
                wait_apart(dve, dve_passed, x1_ready, n + 1)

            def norm_2(n, between=None):
                b = n // TB
                statistics(NT + n, xq[:, n, :])
                if between is not None:
                    rest_of_qz(between)
                wait(dve, sq_ready, n)
                modulate(NT + n, xq[:, n, :], mods[:, CB, b, :], mods[:, SB, b, :])

            def top2(n):
                base = TOP2 * n
                dve.wait_ge(logit_mm, n + 1)
                dve.wait_ge(norm_ready, n + 1)
                nc.vector.tensor_scalar(logit_lo[:], logit_ps[:, LOGITS + E:LOGITS + 2 * E], inv_norm[:, 0:1], None,
                                        ALU.mult).then_inc(top2_step, 1)
                dve.wait_ge(top2_step, base + 1)
                nc.vector.scalar_tensor_tensor(out=logits[:], in0=logit_ps[:, LOGITS:LOGITS + E], scalar=inv_norm[:, 0:1],
                                               in1=logit_lo[:], op0=ALU.mult, op1=ALU.add).then_inc(logits_ready, 1)
                wait_apart(dve, dve_passed, logits_ready, n + 1)
                nc.vector.max(out=top[:], in_=logits[:]).then_inc(top2_step, 1)
                wait_apart(dve, dve_passed, top2_step, base + 2)
                nc.vector.max_index(top_at[:], top[:], logits[:]).then_inc(top2_step, 1)
                dve.wait_ge(top2_step, base + 3)
                nc.vector.tensor_tensor(gap[:], top[:, 1:2], top[:, 0:1], ALU.subtract).then_inc(top2_step, 1)
                nc.vector.tensor_copy(top_at_f[:], top_at[:, 0:2]).then_inc(top2_step, 1)
                dve.wait_ge(ratio_ready, n + 1)
                nc.vector.tensor_scalar(ratio_1[:], ratio[:], 1.0, None, ALU.add).then_inc(top2_step, 1)
                dve.wait_ge(top2_step, base + 6)
                nc.vector.reciprocal(weight[:, 0:1], ratio_1[:]).then_inc(top2_step, 1)
                dve.wait_ge(top2_step, base + 7)
                nc.vector.tensor_tensor(weight[:, 1:2], ratio[:], weight[:, 0:1], ALU.mult).then_inc(top2_step, 1)
                dve.wait_ge(top2_step, base + 8)
                nc.vector.tensor_scalar(combine_0[:], expert_no[:], top_at_f[:, 0:1], weight[:, 0:1],
                                        ALU.is_equal, ALU.mult)
                nc.vector.tensor_scalar(combine_1[:], expert_no[:], top_at_f[:, 1:2], weight[:, 1:2],
                                        ALU.is_equal, ALU.mult).then_inc(top2_step, 1)
                dve.wait_ge(top2_step, base + 9)
                nc.vector.tensor_tensor(combine[:], combine_0[:], combine_1[:], ALU.add).then_inc(top2_step, 1)
                dve.wait_ge(top2_step, base + 10)

            def scale_up(n):
                dve.wait_ge(up_mm, n + 1)
                wait(dve, s_transposed, NB * n)
                for j in range(NB):
                    last = nc.vector.tensor_tensor(
                        s_sb[:, cols(j, C)].rearrange("p (e r) -> p e r", r=R),
                        up_ps[j][:].rearrange("p (e r) -> p e r", r=R),
                        combine[:, j * EPB:(j + 1) * EPB].unsqueeze(2).broadcast_to((P, EPB, R)), ALU.mult)
                last.then_inc(s_ready, 1)

            def rest_of_s(n):
                for j in range(NB):
                    dve.wait_ge(sT_hi_ready, NB * n + j + 1)
                    last = nc.vector.tensor_tensor(sT_lo[:, j * EPB:(j + 1) * EPB, :],
                                                   sT_ps[j][:].rearrange("p (e t) -> p e t", t=P),
                                                   f32(sT_hi[:, j * EPB:(j + 1) * EPB, :]), ALU.subtract)
                last.then_inc(sT_lo_ready, 1)

            def gate_ffn(n):
                dve.wait_ge(ffn_mm, n + 1)
                wait(dve, out_ready, n)
                nc.vector.tensor_tensor(ffn[:], ffn_ps[:], mods[:, GB, n // TB, :], ALU.mult).then_inc(ffn_ready, 1)

            def step(i, has_prev, has_next, has_second, has_third):
                top2(i)
                scale_up(i)
                if has_next:
                    add_attention(i + 1)
                    norm_2(i + 1, i + 2 if has_second else None)
                if has_prev:
                    gate_ffn(i - 1)
                if has_next:
                    rest_of_hT(NT + i + 1)
                if has_third:
                    normalise_q(i + 3)
                rest_of_s(i)

            dve.wait_ge(ksum_ready, 1)
            normalise_q(0)
            phi_k(NT - 1)
            rest_of_qz(0)
            phi_q(NT - 1)
            mask_kv(1)
            normalise_q(1)
            add_attention(0)
            norm_2(0, 1)
            rest_of_m(1)
            rest_of_hT(NT)
            add_attention(1)
            norm_2(1)
            normalise_q(2)
            top2(0)
            scale_up(0)
            rest_of_qz(2)
            rest_of_s(0)
            rest_of_hT(NT + 1)
            normalise_q(3)
            for g in range(2):
                e = slice(g * E // 2, (g + 1) * E // 2)
                dve.wait_ge(wb_hi_ready, g + 1)
                nc.vector.tensor_tensor(wb_lo[:, e, :], wb_raw[:, e, :], f32(wb_hi[:, e, :]),
                                        ALU.subtract).then_inc(wb_ready, 1)
            dve.wait_ge(ksum_ready, B)
            step(1, True, True, True, True)
            with dve.Fori(2, NT - 3) as i:
                step(i, True, True, True, True)
            for i in range(NT - 3, NT):
                step(i, True, i + 1 < NT, i + 2 < NT, i + 3 < NT)
            gate_ffn(NT - 1)
            dve.wait_ge(ffn_ready, NT)
            nc.vector.tensor_tensor(xq[:, NT - 1, :], xq[:, NT - 1, :], ffn[:], ALU.add).then_inc(last_out_ready, 1)

        @block.tensor
        def _(pe):
            mm = nc.tensor.matmul

            def sum_mod(d, b):
                pe.wait_ge(mod_acc_ready, d + 1)
                if not isinstance(d, int) or d >= B:
                    pe.wait_ge(mod_ready, d + 1)
                mm(mod_ps[b][:], ones[:], mod_acc[b][:], start=True, stop=True).then_inc(mod_mm, 1)

            def mod_direct(n, chunks, arrived):
                for k in chunks:
                    if k % (KC // 2) == 0:
                        pe.wait_ge(arrived[k // (KC // 2)], 16)
                    last = mm(direct_ps[n][:], silu_wide[:, k, :], wmod_raw[:, n, k, :], start=(k == 0), stop=(k == KC - 1))
                return last

            def transpose_h(m):
                pe.wait_ge(h_ready, m + 1)
                for k in range(KC):
                    last = nc.tensor.transpose(hT_ps[:, cols(k)], h[:, cols(k)], ident[:])
                last.then_inc(h_transposed, 1)

            def project(dst, hi, lo, w_hi_of, w_lo_of, lo_ready=None, w_lo_ready=None):
                passes = [(hi, w_hi_of, None), (hi, w_lo_of, w_lo_ready), (lo, w_hi_of, lo_ready)]
                if w_lo_ready is not None:
                    passes = [passes[0], passes[2], passes[1]]
                for part, w_of, ready in passes:
                    if ready is not None:
                        pe.wait_ge(*ready)
                    for k in range(KC):
                        last = mm(dst, part[:, cols(k)], w_of(k), start=(part is hi and w_of is w_hi_of and k == 0),
                                  stop=(part is passes[2][0] and w_of is passes[2][1] and k == KC - 1))
                return last

            def project_h(j, dst, **ready):
                return project(dst[:], hT_hi, hT_lo, lambda k: w_hi[:, j, k, :], lambda k: w_lo[:, j, k, :], **ready)

            pe.wait_ge(const_ready, CONSTANTS)
            pe.wait_ge(silu_wide_ready, 1)
            mod_direct(CA, range(KC // 2), ca_in)
            sum_mod(0, 0)
            mod_direct(CA, range(KC // 2, KC - 1), ca_in)
            sum_mod(1, 1)
            mod_direct(CA, range(KC - 1, KC), ca_in).then_inc(mod_mm, 1)
            mod_direct(SA, range(KC // 2), sa_in)
            pe.wait_ge(ident_ready, 1)
            transpose_h(0)
            mod_direct(SA, range(KC // 2, KC), sa_in).then_inc(mod_mm, 1)

            def times_k(i):
                pe.wait_ge(hT_hi_ready, i + 1)
                wait(pe, k_parts, i)
                first = isinstance(i, int) and i == 0
                if first:
                    pe.wait_ge(w_hi_ready, 1)
                project_h(K, k_ps, lo_ready=(hT_lo_ready, i + 1), w_lo_ready=(w_lo_ready, 1) if first else None).then_inc(k_mm, 1)

            def times_v(i):
                wait(pe, v_ready, i)
                first = isinstance(i, int) and i == 0
                if first:
                    pe.wait_ge(w_hi_ready, 2)
                project_h(V, v_ps, w_lo_ready=(w_lo_ready, 2) if first else None).then_inc(v_mm, 1)

            def times_q(i):
                wait(pe, q_parts, i)
                first = isinstance(i, int) and i == 0
                if first:
                    pe.wait_ge(w_hi_ready, 3)
                project_h(Q, q_ps, w_lo_ready=(w_lo_ready, 3) if first else None).then_inc(q_mm, 1)

            def add_kv(i, t):
                pe.wait_ge(k_ready, i + 1)
                pe.wait_ge(v_ready, i + 1)
                if t == 0:
                    pe.wait_ge(mod_ready, 4)
                    wait(pe, kv_ready, i // TB)
                    wait(pe, m_ready, i // TB * KC)
                for j in range(KC):
                    last = mm(kv_ps[:, cols(j)], v_sb[:, cols(j)], k_sb[:, cols(j)],
                              start=(t == 0 and j == 0), stop=(t == TB - 1), skip_group_check=True)
                last.then_inc(kv_mm, 1)

            def rest_of_tile(i, t=None, d=None):
                if d is not None:
                    for b in range(B):
                        sum_mod(d + b, b)
                times_v(i)
                transpose_h(i + 1)
                if isinstance(i, int) and i == TB:
                    pe.wait_ge(m_ready, KC)
                times_q(i)
                add_kv(i, t)

            def tile(i, t=None, d=None):
                times_k(i)
                rest_of_tile(i, t, d)

            def sum_k(b):
                pe.wait_ge(k_added, (b + 1) * TB)
                wait(pe, ksum_ready, b)
                mm(ksum_ps[:], ones[:], k_acc[:], start=True, stop=True).then_inc(ksum_mm, 1)

            def make_m(b):
                pe.wait_ge(wo_gated, b + 1)
                pe.wait_ge(q_parts, (b + 1) * TB)
                pe.wait_ge(v_ready, (b + 1) * TB)
                pe.wait_ge(kv_ready, b + 1)
                wait(pe, m_ready, b * KC)
                for j in range(KC):
                    mm(m_ps[b][j][:], kv_sb[:, cols(j)], wo_f[:, j, :], start=True, stop=True).then_inc(m_mm, 1)

            times_k(0)
            times_v(0)
            times_q(0)
            transpose_h(1)
            add_kv(0, 0)
            tile(1)
            with pe.Fori(2, 6) as t:
                tile(t, None, B * (t - 1))
            tile(TB - 2)
            tile(TB - 1, TB - 1)
            sum_k(0)
            times_k(TB)
            make_m(0)
            rest_of_tile(TB, 0)
            with pe.Fori(TB + 1, NT - 1) as i:
                tile(i)

            def transpose_qz(n, bank_read):
                pe.wait_ge(qz_ready, n + 1)
                if bank_read is not None:
                    pe.wait_ge(*bank_read)
                for k in range(KC):
                    last = nc.tensor.transpose(t_ps[:, cols(k)], qz[:, cols(k)], ident[:])
                last.then_inc(qz_transposed, 1)

            def attention(n):
                b = n // TB
                pe.wait_ge(qzT_hi_ready, n + 1)
                wait(pe, x1_ready, n)
                project(attn_ps[:], qzT_hi, qzT_lo, lambda k: m_hi[:, b, k, :], lambda k: m_lo[:, b, k, :],
                        lo_ready=(qzT_lo_ready, n + 1)).then_inc(attn_mm, 1)

            def experts_up(i):
                pe.wait_ge(hT_hi_ready, NT + i + 1)
                wait(pe, logits_ready, i)
                wait(pe, s_ready, i)
                for k in range(KC):
                    for j in range(NB):
                        mm(up_ps[j][:], hT_hi[:, cols(k)], wa_hi[:, k, cols(j, C)], start=(k == 0), stop=False)
                        mm(up_ps[j][:], hT_hi[:, cols(k)], wa_lo[:, k, cols(j, C)], start=False, stop=False)
                    if k == 1:
                        pe.wait_ge(hT_lo_ready, NT + i + 1)
                        for c in range(KC):
                            for part in (hT_hi, hT_lo):
                                last = mm(logit_ps[0:2 * E, 0:P], router_2[:, c, :], part[:, cols(c)],
                                          start=(c == 0 and part is hT_hi), stop=(c == KC - 1 and part is hT_lo))
                        last.then_inc(logit_T_mm, 1)
                wait_apart(pe, pe_passed, logits_T_ready, i + 1)
                nc.tensor.transpose(logit_ps[:, LOGITS:LOGITS + 2 * E], logits_T[:], ident[0:2 * E, 0:2 * E]).then_inc(logit_mm, 1)
                for k in range(KC):
                    for j in range(NB):
                        last = mm(up_ps[j][:], hT_lo[:, cols(k)], wa_hi[:, k, cols(j, C)], start=False, stop=(k == KC - 1))
                last.then_inc(up_mm, 1)

            def experts_down(n):
                wait(pe, ffn_ready, n)
                for e in range(E):
                    if e % EPB == 0:
                        pe.wait_ge(sT_hi_ready, NB * n + e // EPB + 1)
                    mm(ffn_ps[:], sT_hi[:, e, :], wb_hi[:, e, :], start=(e == 0), stop=False)
                    mm(ffn_ps[:], sT_hi[:, e, :], wb_lo[:, e, :], start=False, stop=False)
                pe.wait_ge(sT_lo_ready, n + 1)
                for e in range(E):
                    last = mm(ffn_ps[:], sT_lo[:, e, :], wb_hi[:, e, :], start=False, stop=(e == E - 1))
                last.then_inc(ffn_mm, 1)

            def transpose_s(i):
                pe.wait_ge(s_ready, i + 1)
                wait(pe, sT_lo_ready, i)
                for e in range(E):
                    last = nc.tensor.transpose(sT_ps[e // EPB][:, cols(e % EPB)], s_sb[:, cols(e)], ident[:])
                    if e % EPB == EPB - 1:
                        last.then_inc(s_transposed, 1)

            def first_step():
                experts_up(0)
                transpose_qz(2, (hT_lo_ready, NT + 1))
                transpose_s(0)
                pe.wait_ge(qzT_lo_ready, 3)
                transpose_h(NT + 1)

            def step(i, has_prev, has_next, has_second):
                experts_up(i)
                if has_second:
                    transpose_qz(i + 2, (hT_lo_ready, NT + i + 1))
                if has_next:
                    attention(i + 1)
                if has_prev:
                    if isinstance(i, int) and i == 1:
                        pe.wait_ge(wb_ready, 2)
                    experts_down(i - 1)
                if has_next:
                    if has_second:
                        pe.wait_ge(qzT_lo_ready, i + 3)
                    transpose_h(NT + i + 1)
                transpose_s(i)

            times_k(NT - 1)
            times_v(NT - 1)
            transpose_qz(0, (hT_lo_ready, NT))
            times_q(NT - 1)
            add_kv(NT - 1, TB - 1)
            sum_k(1)
            pe.wait_ge(m_ready, KC)
            pe.wait_ge(q_parts, NT)
            attention(0)
            transpose_qz(1, (qzT_lo_ready, 1))
            make_m(1)
            pe.wait_ge(qzT_lo_ready, 2)
            transpose_h(NT)
            attention(1)
            pe.wait_ge(router_ready, 1)
            pe.wait_ge(wa_ready, TB)
            pe.wait_ge(m_ready, B * KC)
            first_step()
            step(1, True, True, True)
            with pe.Fori(2, NT - 3) as i:
                step(i, True, True, True)
            for i in range(NT - 3, NT):
                step(i, True, i + 1 < NT, i + 2 < NT)
            experts_down(NT - 1)


def kernel(L0_attn_x, L0_attn_cos, L0_attn_sin, L0_attn_Wq, L0_attn_Wk, L0_attn_Wv, L0_attn_Wo,
           L0_ffn_router_w, L0_ffn_Wa, L0_ffn_Wb, L0_c, L0_wmod):
    import concourse.bacc as bacc
    import numpy as np
    from concourse.bass_utils import run_bass_kernel_spmd

    def dense(a):
        return np.ascontiguousarray(a)

    x = np.asarray(L0_attn_x)
    c = np.asarray(L0_c)
    experts, features, rank = L0_ffn_Wa.shape
    chunks = features // P
    arrays = {
        "x": dense(x.reshape(-1, features)),
        "c_cols": dense(c.T.reshape(chunks, P, -1).transpose(1, 0, 2)),
        "wq": dense(np.asarray(L0_attn_Wq).T),
        "wk": dense(np.asarray(L0_attn_Wk).T),
        "wv": dense(np.asarray(L0_attn_Wv).T),
        "wo": dense(np.asarray(L0_attn_Wo).T),
        "router": dense(np.asarray(L0_ffn_router_w).reshape(chunks, P, -1).transpose(1, 0, 2)),
        "wa": dense(np.asarray(L0_ffn_Wa).transpose(1, 0, 2).reshape(features, experts * rank)),
        "wb": dense(L0_ffn_Wb),
        "wmod": dense(L0_wmod),
    }
    nc = bacc.Bacc("TRN2", target_bir_lowering=False, num_devices=1)
    args = [nc.dram_tensor(name, a.shape, mybir.dt.from_np(a.dtype), kind="ExternalInput").ap()
            for name, a in arrays.items()]
    out = nc.dram_tensor("out", arrays["x"].shape, F32, kind="ExternalOutput").ap()
    adaln_block(nc, *args, out)
    result = run_bass_kernel_spmd(nc, [arrays], core_ids=[0])
    return result.results[0]["out"].reshape(x.shape)
```

```python
from contextlib import ExitStack

import concourse.bass as bass
from concourse import mybir

ALU = mybir.AluOpType
ACT = mybir.ActivationFunctionType
AX = mybir.AxisListType
F32 = mybir.dt.float32
F32R = mybir.dt.float32r
U32 = mybir.dt.uint32

P = 128
LN_EPS = 1e-5
DEN_EPS = 1e-6
NORM_FLOOR = 1e-12
GATE_FLOOR = 0.25
KB = 1024
CA, SA, SB, CB, GA, GB = range(6)
IN_WMOD = [1, 0, 3, 4, 2, 5]
Q, K, V = range(3)


def adaln_block(nc, x, c_cols, wq, wk, wv, wo, router, wa, wb, wmod, out):
    TOK, C = x.shape
    B = c_cols.shape[2]
    E, R, _ = wb.shape
    KC = C // P
    NT = TOK // P
    TB = NT // B
    DH = 32
    H = C // DH
    NB = E * R // C
    EPB = E // NB
    assert C == 512 and R == P and E == 8 and NT * P == TOK and TB * B == NT and TB == KC * NB == 8 and B == 2

    x_t = x.rearrange("(n p) c -> p n c", p=P)
    out_t = out.rearrange("(n p) c -> p n c", p=P)

    def chunked(w):
        return w.rearrange("(k p) n -> p k n", p=P)

    BASE = 16512
    ROW = C * 4
    WQKV_AT = BASE
    WO_AT = WQKV_AT + 2 * 3 * KC * ROW
    XQ_AT = WO_AT + KC * ROW
    U_AT = XQ_AT + NT * ROW
    WA_AT = U_AT + 2 * B * KC * ROW
    MODS_AT = WA_AT + 2 * KC * NB * ROW
    STAGE_AT = MODS_AT + 6 * B * ROW
    SMALL_AT = STAGE_AT + 13 * ROW

    def at(name, shape, dt, offset):
        return nc.alloc_sbuf_tensor_at(name, shape, dt, offset=offset)

    w_hi = at("w_hi", [P, 3, KC, C], F32R, WQKV_AT)
    w_lo = at("w_lo", [P, 3, KC, C], F32R, WQKV_AT + 3 * KC * ROW)
    wb_hi = at("wb_hi", [P, E, C], F32R, WQKV_AT)
    wb_lo = at("wb_lo", [P, E, C], F32R, WQKV_AT + E * ROW)
    wo_f = at("wo_f", [P, KC, C], F32, WO_AT)
    sT_hi = at("sT_hi", [P, E, P], F32R, WO_AT)
    sT_lo = at("sT_lo", [P, E, P], F32R, WO_AT + 2 * ROW)
    xq = at("xq", [P, NT, C], F32, XQ_AT)
    m_hi = at("m_hi", [P, B, KC, C], F32R, U_AT)
    m_lo = at("m_lo", [P, B, KC, C], F32R, U_AT + B * KC * ROW)
    wa_hi = at("wa_hi", [P, KC, E * R], F32R, WA_AT)
    wa_lo = at("wa_lo", [P, KC, E * R], F32R, WA_AT + KC * NB * ROW)
    wmod_raw = at("wmod_raw", [P, 6, KC, C], F32, U_AT)
    raw = at("w_raw", [P, 3, KC, C], F32, WQKV_AT + 3 * KC * ROW)
    wb_raw = at("wb_raw", [P, E, C], F32, WQKV_AT + E * ROW)
    wa_raw = at("wa_raw", [P, KC, E * R], F32, WA_AT + KC * NB * ROW)
    mods = at("mods", [P, 6, B, C], F32, MODS_AT)

    def stage(name, n, dt=F32, rows=1, shape=None):
        return at(name, shape or [P, rows * C], dt, STAGE_AT + n * ROW)

    h = stage("h", 0)
    hT_hi = stage("hT_hi", 1, F32R)
    hT_lo = stage("hT_lo", 2, F32R)
    exp_k, relu_k = stage("exp_k", 3), stage("relu_k", 4)
    exp_q, relu_q = stage("exp_q", 5), stage("relu_q", 6)
    k_sb, v_sb = stage("k_sb", 7), stage("v_sb", 8)
    k_acc = stage("k_acc", 9)
    kv_sb = stage("kv_sb", 10)
    mod_acc = [stage("mod_acc0", 11), stage("mod_acc1", 12)]
    silu_wide = at("silu_wide", [P, KC, P], F32, STAGE_AT + 9 * ROW)
    mod_acc_hi = [at(f"mod_acc_hi{b}", [P, C], F32R, MODS_AT + (GB * B + b) * ROW) for b in range(B)]
    mod_acc_lo = [stage(f"mod_acc_lo{b}", 11 + b, F32R) for b in range(B)]
    gate_sign = at("gate_sign", [P, C], F32, STAGE_AT + 10 * ROW)
    qzT_hi, qzT_lo = stage("qzT_hi", 3, F32R), stage("qzT_lo", 4, F32R)
    s_sb = stage("s_sb", 7, rows=NB)
    q_ksum = at("q_ksum", [P, C], F32, MODS_AT + (SA * B + 0) * ROW)
    qz = at("qz", [P, C], F32, MODS_AT + (SA * B + 1) * ROW)
    square = at("square", [P, C], F32, MODS_AT + (GA * B + 0) * ROW)
    ffn = at("ffn", [P, C], F32, MODS_AT + (GA * B + 1) * ROW)

    small_end = [SMALL_AT]

    def small(name, shape, dt=F32):
        n = 1
        for d in shape[1:]:
            n *= d
        t = at(name, shape, dt, small_end[0])
        small_end[0] += -(-n * 4 // 32) * 32
        return t

    ident = small("ident", [P, P])
    ones = small("ones", [P, P])
    ones_r = small("ones_r", [P, P], F32R)
    head_mask = small("head_mask", [P, P])
    router_raw = small("router_raw", [P, KC, E])
    router_2 = small("router_2", [P, KC, 2 * E], F32R)
    c_sb = small("c_sb", [P, KC, B])
    exp_c = small("exp_c", [P, KC, B])
    silu_c = small("silu_c", [P, KC, B])
    minus_half = small("minus_half", [P, 1])
    mod_bias = small("mod_bias", [P, 6])
    logits_T = small("logits_T", [2 * E, P])
    expert_no = small("expert_no", [P, E])
    bn6 = small("bn6", [P, 6])
    mean_var = small("mean_var", [P, 2])
    var_eps = small("var_eps", [P, 1])
    rstd = small("rstd", [P, 1])
    den = small("den", [P, H])
    den_eps = small("den_eps", [P, H])
    z = small("z", [P, H])
    sq_sum = small("sq_sum", [P, 1])
    sq_floor = small("sq_floor", [P, 1])
    inv_norm = small("inv_norm", [P, 1])
    logit_lo = small("logit_lo", [P, E])
    logits = small("logits", [P, E])
    top = small("top", [P, 8])
    top_at = small("top_at", [P, 8], U32)
    top_at_f = small("top_at_f", [P, 2])
    gap = small("gap", [P, 1])
    ratio = small("ratio", [P, 1])
    ratio_1 = small("ratio_1", [P, 1])
    weight = small("weight", [P, 2])
    combine_0 = small("combine_0", [P, E])
    combine_1 = small("combine_1", [P, E])
    combine = small("combine", [P, E])

    with ExitStack() as ctx:
        banks = [ctx.enter_context(nc.psum_tensor(f"bank{n}", [P, C], F32)) for n in range(8)]
        k_ps, v_ps, q_ps, hT_ps, kv_ps, ksum_ps = banks[:6]
        mod_ps = banks[6:8]
        direct_ps = {CA: ksum_ps, SA: kv_ps}
        m_ps = [banks[6:8] + [q_ps, kv_ps], banks[6:8] + [k_ps, v_ps]]
        up_ps = banks[0:2]
        attn_ps, t_ps, ffn_ps, logit_ps = banks[2:6]
        sT_ps = banks[6:8]
        last_ps = [ffn_ps, attn_ps]

        def sem(name):
            return ctx.enter_context(nc.semaphore(name))

        c_in, wo_in, router_in, wa_in, wb_in = (sem(s) for s in ("c_in", "wo_in", "router_in", "wa_in", "wb_in"))
        ca_in, sa_in = ([sem(f"{row}_in{g}") for g in range(2)] for row in ("ca", "sa"))
        sb_in, wmod_in = sem("sb_in"), sem("wmod_in")
        w_in = {j: sem(f"w_in{j}") for j in (Q, K, V)}
        x_in = [sem(f"x_in{n}") for n in range(4)]
        x_again = sem("x_again")
        out_done = sem("out_done")
        const_step, const_ready, ident_ready = sem("const_step"), sem("const_ready"), sem("ident_ready")
        c_exp, silu_step, silu_ready, silu_wide_ready = (sem(s) for s in ("c_exp", "silu_step", "silu_ready", "silu_wide_ready"))
        mod_step, mod_acc_ready, mod_mm, mod_ready = (sem(s) for s in ("mod_step", "mod_acc_ready", "mod_mm", "mod_ready"))
        mod_begun, mod_hi_ready, mod_lo_ready = sem("mod_begun"), sem("mod_hi_ready"), sem("mod_lo_ready")
        gate_step, gates_ready, wo_gated = sem("gate_step"), sem("gates_ready"), sem("wo_gated")
        w_hi_ready, w_lo_ready = sem("w_hi_ready"), sem("w_lo_ready")
        router_hi_ready, router_ready = sem("router_hi_ready"), sem("router_ready")
        wa_hi_ready, wa_ready = sem("wa_hi_ready"), sem("wa_ready")
        wb_hi_ready, wb_ready = sem("wb_hi_ready"), sem("wb_ready")
        bn_ready, stats_ready, var_ready, rstd_ready = (sem(s) for s in ("bn_ready", "stats_ready", "var_ready", "rstd_ready"))
        scaled_ready, h_ready = sem("scaled_ready"), sem("h_ready")
        h_transposed, hT_hi_ready, hT_lo_ready = (sem(s) for s in ("h_transposed", "hT_hi_ready", "hT_lo_ready"))
        k_mm, v_mm, q_mm, kv_mm = (sem(s) for s in ("k_mm", "v_mm", "q_mm", "kv_mm"))
        k_parts, q_parts = sem("k_parts"), sem("q_parts")
        k_ready, v_ready, q_ready, k_added = (sem(s) for s in ("k_ready", "v_ready", "q_ready", "k_added"))
        ksum_mm, ksum_ready, kv_ready = sem("ksum_mm"), sem("ksum_ready"), sem("kv_ready")
        m_mm, m_hi_ready, m_ready = sem("m_mm"), sem("m_hi_ready"), sem("m_ready")
        q_ksum_ready, den_step, qz_ready, qz_transposed = (sem(s) for s in ("q_ksum_ready", "den_step", "qz_ready", "qz_transposed"))
        qzT_hi_ready, qzT_lo_ready = sem("qzT_hi_ready"), sem("qzT_lo_ready")
        attn_mm, x1_ready = sem("attn_mm"), sem("x1_ready")
        sq_ready, sq_floored, norm_ready = sem("sq_ready"), sem("sq_floored"), sem("norm_ready")
        logit_T_mm, logits_T_ready = sem("logit_T_mm"), sem("logits_T_ready")
        logit_mm, logits_ready, top2_step, ratio_ready = (sem(s) for s in ("logit_mm", "logits_ready", "top2_step", "ratio_ready"))
        up_mm, s_ready, s_transposed = sem("up_mm"), sem("s_ready"), sem("s_transposed")
        sT_hi_ready, sT_lo_ready = sem("sT_hi_ready"), sem("sT_lo_ready")
        ffn_mm, ffn_ready, out_ready, last_out_ready = (sem(s) for s in ("ffn_mm", "ffn_ready", "out_ready", "last_out_ready"))

        sp_passed, pool_passed, dve_passed, act_passed, pe_passed = (
            sem(s) for s in ("sp_passed", "pool_passed", "dve_passed", "act_passed", "pe_passed"))

        def wait(eng, s, value):
            if not (isinstance(value, int) and value <= 0):
                eng.wait_ge(s, value)

        def wait_apart(eng, passed, s, value):
            wait(eng, s, value)
            if not isinstance(value, int):
                eng.sem_inc(passed, 1)

        def cols(j, width=P):
            return slice(j * width, (j + 1) * width)

        def f32(t):
            return t.bitcast(F32)

        LOGITS = 2 * P
        CONSTANTS = 7 + P // DH + E
        TOP2 = 10

        block = ctx.enter_context(nc.Block())

        @block.sync
        def _(sp):
            def load_wmod(n):
                j = IN_WMOD[n]
                return sp.dma_start(wmod_raw[:, n, :, :], chunked(wmod[:, cols(j, C)]))

            def load_wo(b):
                return sp.dma_start(wo_f[:], chunked(wo)).then_inc(wo_in, 16)

            sp.dma_start(c_sb[:], c_cols).then_inc(c_in, 16)
            for n, arrived in ((CA, ca_in), (SA, sa_in)):
                for g in range(2):
                    k = slice(g * KC // 2, (g + 1) * KC // 2)
                    sp.dma_start(wmod_raw[:, n, k, :], chunked(wmod[:, cols(IN_WMOD[n], C)])[:, k, :]).then_inc(arrived[g], 16)
            sp.dma_start(xq[:, 0, :], x_t[:, 0, :]).then_inc(x_in[0], 16)
            for j, w in ((K, wk), (V, wv), (Q, wq)):
                sp.dma_start(raw[:, j, :, :], chunked(w)).then_inc(w_in[j], 16)
                if j == V:
                    sp.dma_start(xq[:, 1, :], x_t[:, 1, :]).then_inc(x_in[1], 16)
            load_wmod(SB).then_inc(sb_in, 16)
            sp.dma_start(xq[:, 2:TB, :], x_t[:, 2:TB, :]).then_inc(x_in[2], 16)
            for n in (CB, GA, GB):
                load_wmod(n).then_inc(wmod_in, 16)
            load_wo(0)
            sp.dma_start(router_raw[:], router).then_inc(router_in, 16)
            sp.dma_start(wa_raw[:], chunked(wa)).then_inc(wa_in, 16)
            sp.dma_start(xq[:, TB:NT, :], x_t[:, TB:NT, :]).then_inc(x_in[3], 16)
            sp.wait_ge(m_mm, KC)
            load_wo(1)
            def reload_x(n):
                sp.wait_ge(qz_ready, n + 1)
                sp.dma_start(xq[:, n, :], x_t[:, n, :]).then_inc(x_again, 16)
                wait_apart(sp, sp_passed, x_again, 16 * (n + 1))

            def store(n):
                sp.wait_ge(out_ready, n + 1)
                sp.dma_start(out_t[:, n, :], xq[:, n, :]).then_inc(out_done, 16)

            reload_x(0)
            sp.wait_ge(q_mm, NT)
            sp.dma_start(wb_raw[:], wb.rearrange("e r c -> r e c")).then_inc(wb_in, 16)
            LAG = 4
            with sp.Fori(1, LAG) as n:
                reload_x(n)
            with sp.Fori(LAG, NT) as n:
                reload_x(n)
                store(n - LAG)
            with sp.Fori(NT - LAG, NT - 1) as n:
                store(n)
            for g in range(2):
                sp.wait_ge(last_out_ready, g + 1)
                half = cols(g, C // 2)
                sp.dma_start(out_t[:, NT - 1, half], xq[:, NT - 1, half]).then_inc(out_done, 16)
            sp.wait_ge(out_done, 16 * (NT + 1))

        @block.gpsimd
        def _(pool):
            nc.gpsimd.memset(ident[:], 1.0).then_inc(const_step, 1)
            pool.wait_ge(const_step, 1)
            nc.gpsimd.affine_select(out=ident[:], in_=ident[:], compare_op=ALU.is_equal, fill=0.0, base=0,
                                    pattern=[[-1, P]], channel_multiplier=1).then_inc(ident_ready, 1)
            pool.wait_ge(ident_ready, 1)
            pool.wait_ge(const_ready, CONSTANTS)

            def inverse_std(m):
                pool.wait_ge(stats_ready, m + 1)
                wait_apart(pool, pool_passed, h_ready, m)
                nc.gpsimd.tensor_scalar(var_eps[:], mean_var[:, 1:2], LN_EPS, None, ALU.add).then_inc(var_ready, 1)
                pool.wait_ge(var_ready, m + 1)
                nc.gpsimd.tensor_tensor(rstd[:], var_eps[:], minus_half[:], ALU.pow).then_inc(rstd_ready, 1)

            inverse_std(0)

            def add_k(i, first):
                pool.wait_ge(k_ready, i + 1)
                if first:
                    wait(pool, ksum_mm, i // TB)
                    nc.gpsimd.tensor_copy(k_acc[:], k_sb[:]).then_inc(k_added, 1)
                else:
                    pool.wait_ge(k_added, i)
                    nc.gpsimd.tensor_tensor(k_acc[:], k_acc[:], k_sb[:], ALU.add).then_inc(k_added, 1)

            def split_wa(t):
                here = cols(t, C) if isinstance(t, int) else bass.ts(t, C)
                hi, lo, src = (w[:].rearrange("p k n -> p (k n)")[:, here] for w in (wa_hi, wa_lo, wa_raw))
                nc.gpsimd.tensor_copy(hi, src).then_inc(wa_hi_ready, 1)
                wait_apart(pool, pool_passed, wa_hi_ready, t + 1)
                nc.gpsimd.tensor_tensor(lo, src, f32(hi), ALU.subtract).then_inc(wa_ready, 1)

            def gate_wo(b):
                pool.wait_ge(wo_in, 16 * (b + 1))
                pool.wait_ge(gates_ready, 2)
                nc.gpsimd.tensor_tensor(wo_f[:], wo_f[:], mods[:, GA, b, :].unsqueeze(1).broadcast_to((P, KC, C)),
                                        ALU.mult).then_inc(wo_gated, 1)

            def rest_of_mod(d, b):
                pool.wait_ge(mod_hi_ready, d + 1 - B)
                nc.gpsimd.tensor_tensor(mod_acc_lo[b][:], mod_acc[b][:], f32(mod_acc_hi[b][:]),
                                        ALU.subtract).then_inc(mod_lo_ready, 1)

            for b in range(B):
                i = b * TB
                inverse_std(i + 1)
                if b == 0:
                    add_k(0, True)
                    inverse_std(2)
                    for e in range(B):
                        rest_of_mod(B + e, e)
                    with pool.Fori(2, GA + 1) as t:
                        add_k(t - 1, False)
                        inverse_std(t + 1)
                        for e in range(B):
                            rest_of_mod(B * t + e, e)
                    inverse_std(GA + 2)
                    for t in (GA, GA + 1):
                        add_k(t, False)
                if b == 1:
                    add_k(i, True)
                    pool.wait_ge(wa_in, 16)
                    pool.wait_ge(mod_acc_ready, 6 * B - 2)
                    split_wa(0)
                    with pool.Fori(1, TB - 2) as t:
                        inverse_std(i + t + 1)
                        add_k(i + t, False)
                        split_wa(t)
                for t in (TB - 2, TB - 1):
                    i = b * TB + t
                    if i + 1 < NT:
                        inverse_std(i + 1)
                    if t == TB - 2:
                        gate_wo(b)
                    add_k(i, False)
                    if b == 1:
                        split_wa(t)

            def inverse_norm(n):
                pool.wait_ge(sq_ready, n + 1)
                wait_apart(pool, pool_passed, logits_ready, n)
                nc.gpsimd.tensor_scalar(sq_floor[:], sq_sum[:], NORM_FLOOR * NORM_FLOOR, None, ALU.max).then_inc(sq_floored, 1)
                pool.wait_ge(sq_floored, n + 1)
                nc.gpsimd.tensor_tensor(inv_norm[:], sq_floor[:], minus_half[:], ALU.pow).then_inc(norm_ready, 1)

            def add_ffn(n):
                pool.wait_ge(ffn_ready, n + 1)
                nc.gpsimd.tensor_tensor(xq[:, n, :], xq[:, n, :], ffn[:], ALU.add).then_inc(out_ready, 1)

            def step(i, has_prev, has_next):
                if has_next:
                    inverse_std(NT + i + 1)
                    inverse_norm(i + 1)
                if has_prev:
                    add_ffn(i - 1)

            inverse_std(NT)
            inverse_norm(0)
            step(0, False, True)
            for g in range(2):
                e = slice(g * E // 2, (g + 1) * E // 2)
                pool.wait_ge(wb_hi_ready, g + 1)
                nc.gpsimd.tensor_tensor(wb_lo[:, e, :], wb_raw[:, e, :], f32(wb_hi[:, e, :]),
                                        ALU.subtract).then_inc(wb_ready, 1)
            with pool.Fori(1, NT - 3) as i:
                step(i, True, True)
            for i in range(NT - 3, NT):
                step(i, True, i + 1 < NT)

        @block.scalar
        def _(act):
            act.wait_ge(c_in, 16)
            nc.scalar.activation(exp_c[:], c_sb[:], ACT.Exp, scale=-1.0).then_inc(c_exp, 1)

            def split_w(j):
                act.wait_ge(w_in[j], 16)
                nc.scalar.activation(w_hi[:, j, :, :], raw[:, j, :, :], ACT.Copy).then_inc(w_hi_ready, 1)

            def spread_mod(u, bank, n, b):
                wait_apart(act, act_passed, mod_mm, u + 1)
                nc.scalar.activation(mods[:, n, b, :], bank[:], ACT.Identity,
                                     bias=mod_bias[:, bass.ds(n, 1)]).then_inc(mod_ready, 1)

            def split_hT(m, last_read=None):
                act.wait_ge(h_transposed, m + 1)
                if last_read is not None:
                    act.wait_ge(*last_read)
                for g in range(2):
                    nc.scalar.activation(hT_hi[:, cols(g, C // 2)], hT_ps[:, cols(g, C // 2)], ACT.Copy).then_inc(hT_hi_ready, 1)

            act.wait_ge(const_ready, CONSTANTS)
            spread_mod(0, mod_ps[0], CA, 0)
            spread_mod(1, mod_ps[1], SA, 0)
            split_w(K)
            split_hT(0)
            split_w(V)
            spread_mod(2, direct_ps[CA], CA, 1)
            spread_mod(3, direct_ps[SA], SA, 1)
            split_w(Q)

            def phi_parts_k(i):
                act.wait_ge(k_mm, i + 1)
                wait(act, k_ready, i)
                nc.scalar.activation(exp_k[:], k_ps[:], ACT.Exp)
                nc.scalar.activation(relu_k[:], k_ps[:], ACT.Relu).then_inc(k_parts, 1)

            def copy_v(i):
                act.wait_ge(v_mm, i + 1)
                wait(act, kv_mm, i)
                nc.scalar.activation(v_sb[:], v_ps[:], ACT.Copy).then_inc(v_ready, 1)

            def phi_parts_q(i):
                act.wait_ge(q_mm, i + 1)
                wait(act, q_ready, i)
                nc.scalar.activation(exp_q[:], q_ps[:], ACT.Exp)
                nc.scalar.activation(relu_q[:], q_ps[:], ACT.Relu).then_inc(q_parts, 1)

            def split_mod(d, b):
                act.wait_ge(mod_acc_ready, d + 1)
                nc.scalar.activation(mod_acc_hi[b][:], mod_acc[b][:], ACT.Copy).then_inc(mod_hi_ready, 1)

            def begin_mod(n):
                for b in range(B):
                    nc.scalar.activation(mod_acc[b][:], wmod_raw[:, n, 0, :], ACT.Copy,
                                         scale=silu_c[:, 0, b:b + 1]).then_inc(mod_begun, 1)

            def tile(i, row=None, k_done=False, d=None):
                if not k_done:
                    phi_parts_k(i)
                if row is not None:
                    for b in range(B):
                        spread_mod(B * row + b, mod_ps[b], row, b)
                if d is not None:
                    begin_mod(i + 1)
                copy_v(i)
                split_hT(i + 1, (q_mm, i + 1))
                if d is not None:
                    split_mod(d, 0)
                if d is not None:
                    split_mod(d + 1, 1)
                phi_parts_q(i)

            def sum_k_out(b):
                act.wait_ge(ksum_mm, b + 1)
                act.wait_ge(h_ready, (b + 1) * TB)
                nc.scalar.activation(mods[:, CA, b, :], ksum_ps[:], ACT.Copy).then_inc(ksum_ready, 1)

            def split_m(b):
                for j in range(KC):
                    act.wait_ge(m_mm, b * KC + j + 1)
                    nc.scalar.activation(m_hi[:, b, j, :], m_ps[b][j][:], ACT.Copy).then_inc(m_hi_ready, 1)

            tile(0)
            act.wait_ge(sb_in, 16)
            tile(1, d=B)
            act.wait_ge(wmod_in, 16 * 3)
            with act.Fori(2, 5) as t:
                tile(t, t, d=B * t)
            tile(GA + 1, GA + 1)
            for i in (TB - 2, TB - 1):
                tile(i)
            sum_k_out(0)
            phi_parts_k(TB)
            split_m(0)
            tile(TB, k_done=True)
            with act.Fori(TB + 1, NT - 1) as i:
                tile(i)

            def split_qz(n):
                act.wait_ge(qz_transposed, n + 1)
                wait(act, attn_mm, n)
                nc.scalar.activation(qzT_hi[:], t_ps[:], ACT.Copy).then_inc(qzT_hi_ready, 1)

            def square_sum(n):
                act.wait_ge(h_ready, NT + n + 1)
                wait(act, norm_ready, n)
                nc.scalar.activation(square[:], h[:], ACT.Square, accum_out=sq_sum[:]).then_inc(sq_ready, 1)

            def copy_logits_T(i):
                act.wait_ge(logit_T_mm, i + 1)
                nc.scalar.activation(logits_T[:], logit_ps[0:2 * E, 0:P], ACT.Copy).then_inc(logits_T_ready, 1)

            def exp_gap(i):
                act.wait_ge(top2_step, TOP2 * i + 4)
                nc.scalar.activation(ratio[:], gap[:], ACT.Exp).then_inc(ratio_ready, 1)

            def split_wb(g):
                act.wait_ge(wb_in, 16)
                e = slice(g * E // 2, (g + 1) * E // 2)
                nc.scalar.activation(wb_hi[:, e, :], wb_raw[:, e, :], ACT.Copy).then_inc(wb_hi_ready, 1)

            def split_sT(i):
                for j in range(NB):
                    act.wait_ge(s_transposed, NB * i + j + 1)
                    nc.scalar.activation(sT_hi[:, j * EPB:(j + 1) * EPB, :], sT_ps[j][:], ACT.Copy).then_inc(sT_hi_ready, 1)

            def first_steps():
                split_wb(0)
                copy_logits_T(0)
                square_sum(1)
                exp_gap(0)
                split_hT(NT + 1)
                split_sT(0)
                split_wb(1)
                copy_logits_T(1)
                split_qz(2)
                exp_gap(1)
                split_qz(3)
                square_sum(2)
                split_hT(NT + 2)
                split_sT(1)

            def step(i, has_next, has_second):
                copy_logits_T(i)
                exp_gap(i)
                if has_second:
                    split_qz(i + 2)
                if has_next:
                    square_sum(i + 1)
                    split_hT(NT + i + 1)
                split_sT(i)

            phi_parts_k(NT - 1)
            copy_v(NT - 1)
            act.wait_ge(k_ready, NT)
            split_qz(0)
            phi_parts_q(NT - 1)
            sum_k_out(1)
            split_qz(1)
            split_m(1)
            split_hT(NT)
            square_sum(0)
            first_steps()
            with act.Fori(2, NT - 3) as i:
                step(i, True, True)
            for i in range(NT - 3, NT):
                step(i, i + 1 < NT, i + 2 < NT)

        @block.vector
        def _(dve):
            nc.vector.memset(head_mask[:], 0.0).then_inc(const_ready, 1)
            dve.wait_ge(const_ready, 1)
            for j in range(P // DH):
                nc.vector.memset(head_mask[cols(j, DH), cols(j, DH)], 1.0).then_inc(const_ready, 1)
            nc.vector.memset(ones[:], 1.0).then_inc(const_ready, 1)
            nc.vector.memset(minus_half[:], -0.5).then_inc(const_ready, 1)
            for e in range(E):
                nc.vector.memset(expert_no[:, e:e + 1], float(e)).then_inc(const_ready, 1)
            nc.vector.memset(mod_bias[:], 0.0).then_inc(const_ready, 1)
            dve.wait_ge(const_ready, CONSTANTS - 3)
            nc.vector.tensor_copy(ones_r[:], ones[:]).then_inc(const_ready, 1)
            for n in (CA, CB):
                nc.vector.memset(mod_bias[:, n:n + 1], 1.0).then_inc(const_ready, 1)
            dve.wait_ge(const_ready, CONSTANTS)
            dve.wait_ge(c_exp, 1)
            nc.vector.tensor_scalar(exp_c[:], exp_c[:], 1.0, None, ALU.add).then_inc(silu_step, 1)
            dve.wait_ge(silu_step, 1)
            nc.vector.reciprocal(exp_c[:], exp_c[:]).then_inc(silu_step, 1)
            dve.wait_ge(silu_step, 2)
            nc.vector.tensor_tensor(silu_c[:], exp_c[:], c_sb[:], ALU.mult).then_inc(silu_ready, 1)
            dve.wait_ge(silu_ready, 1)
            nc.vector.tensor_tensor(silu_wide[:], ones[:].unsqueeze(1).broadcast_to((P, KC, P)),
                                    silu_c[:, :, 1].unsqueeze(2).broadcast_to((P, KC, P)), ALU.mult).then_inc(silu_wide_ready, 1)

            def mod_sums(d, n, entries, arrived=None):
                first = 0 if arrived is not None else 1
                before = (KC - 1) * d if arrived is not None else (KC - 1) * B + (KC - 2) * (d - B)
                for k in range(first, KC):
                    for b in entries:
                        acc = mod_acc[b if arrived is None else d]
                        if arrived is not None and k % (KC // 2) == 0:
                            dve.wait_ge(arrived[k // (KC // 2)], 16)
                        if k == 0:
                            last = nc.vector.tensor_scalar(acc[:], wmod_raw[:, n, k, :], silu_c[:, k, b:b + 1], None, ALU.mult)
                        else:
                            if arrived is None and k == 1:
                                dve.wait_ge(mod_begun, d - B + b + 1)
                            else:
                                dve.wait_ge(mod_step, before + len(entries) * (k - first) + b - len(entries) + 1)
                            last = nc.vector.scalar_tensor_tensor(out=acc[:], in0=wmod_raw[:, n, k, :],
                                                                  scalar=silu_c[:, k, b:b + 1], in1=acc[:],
                                                                  op0=ALU.mult, op1=ALU.add)
                        last.then_inc(mod_step if k < KC - 1 else mod_acc_ready, 1)

            def floor_gate(g, n, b):
                gate = mods[:, n, b, :]
                nc.vector.tensor_scalar(gate_sign[:], gate, 0.0, 2.0, ALU.is_ge, ALU.mult).then_inc(gate_step, 1)
                dve.wait_ge(gate_step, 3 * g + 1)
                nc.vector.tensor_scalar(gate_sign[:], gate_sign[:], -1.0, None, ALU.add).then_inc(gate_step, 1)
                dve.wait_ge(gate_step, 3 * g + 2)
                nc.vector.tensor_tensor(gate, gate, gate_sign[:], ALU.mult).then_inc(gate_step, 1)
                dve.wait_ge(gate_step, 3 * g + 3)
                nc.vector.scalar_tensor_tensor(out=gate, in0=gate, scalar=GATE_FLOOR, in1=gate_sign[:],
                                               op0=ALU.max, op1=ALU.mult).then_inc(gates_ready, 1)
                dve.wait_ge(gates_ready, g + 1)

            def statistics(m, src):
                nc.vector.bn_stats(out=bn6[:], in_=src).then_inc(bn_ready, 1)
                dve.wait_ge(bn_ready, m + 1)
                wait_apart(dve, dve_passed, rstd_ready, m)
                nc.vector.bn_aggr(out=mean_var[:], in_=bn6[:]).then_inc(stats_ready, 1)
                dve.wait_ge(stats_ready, m + 1)

            def modulate(m, src, scale, shift):
                wait(dve, h_transposed, m)
                nc.vector.scalar_tensor_tensor(out=h[:], in0=src, scalar=mean_var[:, 0:1], in1=scale,
                                               op0=ALU.subtract, op1=ALU.mult).then_inc(scaled_ready, 1)
                dve.wait_ge(scaled_ready, m + 1)
                dve.wait_ge(rstd_ready, m + 1)
                nc.vector.scalar_tensor_tensor(out=h[:], in0=h[:], scalar=rstd[:, 0:1], in1=shift,
                                               op0=ALU.mult, op1=ALU.add).then_inc(h_ready, 1)

            def rest_of_hT(m):
                dve.wait_ge(hT_hi_ready, 2 * m + 2)
                nc.vector.tensor_tensor(hT_lo[:], hT_ps[:], f32(hT_hi[:]), ALU.subtract).then_inc(hT_lo_ready, 1)

            def rest_of_w(j, n):
                dve.wait_ge(w_hi_ready, n + 1)
                nc.vector.tensor_tensor(w_lo[:, j, :, :], raw[:, j, :, :], f32(w_hi[:, j, :, :]),
                                        ALU.subtract).then_inc(w_lo_ready, 1)

            mod_sums(0, CA, [0], ca_in)
            mod_sums(1, SA, [0], sa_in)
            dve.wait_ge(x_in[0], 16)
            statistics(0, xq[:, 0, :])
            dve.wait_ge(mod_ready, B)
            modulate(0, xq[:, 0, :], mods[:, CA, 0, :], mods[:, SA, 0, :])
            rest_of_hT(0)
            rest_of_w(K, 0)
            rest_of_w(V, 1)
            dve.wait_ge(x_in[1], 16)
            statistics(1, xq[:, 1, :])
            rest_of_w(Q, 2)
            modulate(1, xq[:, 1, :], mods[:, CA, 0, :], mods[:, SA, 0, :])

            def next_norm(i, b):
                statistics(i, xq[:, i, :])
                modulate(i, xq[:, i, :], mods[:, CA, b, :], mods[:, SA, b, :])

            def phi_k(i):
                dve.wait_ge(k_parts, i + 1)
                wait(dve, k_added, i)
                wait(dve, kv_mm, i)
                nc.vector.scalar_tensor_tensor(out=k_sb[:], in0=exp_k[:], scalar=1.0, in1=relu_k[:],
                                               op0=ALU.min, op1=ALU.add).then_inc(k_ready, 1)

            def phi_q(i):
                dve.wait_ge(q_parts, i + 1)
                nc.vector.scalar_tensor_tensor(out=xq[:, i, :], in0=exp_q[:], scalar=1.0, in1=relu_q[:],
                                               op0=ALU.min, op1=ALU.add).then_inc(q_ready, 1)

            def tile(i, b, d=None, row=None, gates=None):
                next_norm(i + 1, b)
                if gates is not None:
                    dve.wait_ge(mod_ready, B * (gates + GA + 1))
                    floor_gate(B * gates, gates + GA, 0)
                phi_k(i)
                if row is not None:
                    mod_sums(d, row, range(B))
                if gates is not None:
                    floor_gate(B * gates + 1, gates + GA, 1)
                rest_of_hT(i + 1)
                phi_q(i)

            def mask_kv(b):
                dve.wait_ge(kv_mm, (b + 1) * TB)
                wait(dve, m_mm, b * KC)
                nc.vector.tensor_tensor(kv_sb[:].rearrange("p (j e) -> p j e", e=P),
                                        kv_ps[:].rearrange("p (j e) -> p j e", e=P),
                                        head_mask[:].unsqueeze(1).broadcast_to((P, KC, P)),
                                        ALU.mult).then_inc(kv_ready, 1)

            def rest_of_m(b, chunks=range(KC)):
                for j in chunks:
                    dve.wait_ge(m_hi_ready, b * KC + j + 1)
                    nc.vector.tensor_tensor(m_lo[:, b, j, :], m_ps[b][j][:], f32(m_hi[:, b, j, :]),
                                            ALU.subtract).then_inc(m_ready, 1)

            phi_k(0)
            rest_of_hT(1)
            phi_q(0)
            dve.wait_ge(x_in[2], 16)
            dve.wait_ge(sb_in, 16)
            tile(1, 0, B, SB)
            dve.wait_ge(wmod_in, 16 * 3)
            with dve.Fori(2, 5) as t:
                tile(t, 0, B * t, t + 1)
            for g in range(2):
                tile(TB - 3 + g, 0, gates=g)
            dve.wait_ge(router_in, 16)
            nc.vector.tensor_copy(router_2[:, :, 0:E], router_raw[:]).then_inc(router_hi_ready, 1)
            dve.wait_ge(router_hi_ready, 1)
            nc.vector.tensor_tensor(router_2[:, :, E:2 * E], router_raw[:], f32(router_2[:, :, 0:E]),
                                    ALU.subtract).then_inc(router_ready, 1)
            dve.wait_ge(x_in[3], 16)
            tile(TB - 1, 1)
            mask_kv(0)
            next_norm(TB + 1, 1)
            rest_of_m(0)
            phi_k(TB)
            rest_of_hT(TB + 1)
            phi_q(TB)
            with dve.Fori(TB + 1, NT - 1) as i:
                tile(i, 1)

            def normalise_q(n):
                ksum = mods[:, CA, n // TB, :]
                wait(dve, q_ksum_ready, n)
                nc.vector.tensor_tensor(q_ksum[:], xq[:, n, :], ksum, ALU.mult).then_inc(q_ksum_ready, 1)
                dve.wait_ge(q_ksum_ready, n + 1)
                nc.vector.tensor_reduce(den[:], q_ksum[:].rearrange("p (h d) -> p h d", d=DH), AX.X,
                                        ALU.add).then_inc(den_step, 1)
                dve.wait_ge(den_step, 3 * n + 1)
                nc.vector.tensor_scalar(den_eps[:], den[:], DEN_EPS, None, ALU.add).then_inc(den_step, 1)
                dve.wait_ge(den_step, 3 * n + 2)
                nc.vector.reciprocal(z[:], den_eps[:]).then_inc(den_step, 1)
                dve.wait_ge(den_step, 3 * n + 3)
                wait(dve, qz_transposed, n)
                nc.vector.tensor_tensor(qz[:].rearrange("p (h d) -> p h d", d=DH),
                                        xq[:, n, :].rearrange("p (h d) -> p h d", d=DH),
                                        z[:].unsqueeze(2).broadcast_to((P, H, DH)), ALU.mult).then_inc(qz_ready, 1)

            def rest_of_qz(n):
                dve.wait_ge(qzT_hi_ready, n + 1)
                nc.vector.tensor_tensor(qzT_lo[:], t_ps[:], f32(qzT_hi[:]), ALU.subtract).then_inc(qzT_lo_ready, 1)

            def add_attention(n):
                dve.wait_ge(attn_mm, n + 1)
                dve.wait_ge(x_again, 16 * (n + 1))
                nc.vector.tensor_tensor(xq[:, n, :], xq[:, n, :], attn_ps[:], ALU.add).then_inc(x1_ready, 1)
                wait_apart(dve, dve_passed, x1_ready, n + 1)

            def norm_2(n, between=None):
                b = n // TB
                statistics(NT + n, xq[:, n, :])
                if between is not None:
                    rest_of_qz(between)
                wait(dve, sq_ready, n)
                modulate(NT + n, xq[:, n, :], mods[:, CB, b, :], mods[:, SB, b, :])

            def top2(n):
                base = TOP2 * n
                dve.wait_ge(logit_mm, n + 1)
                dve.wait_ge(norm_ready, n + 1)
                nc.vector.tensor_scalar(logit_lo[:], logit_ps[:, LOGITS + E:LOGITS + 2 * E], inv_norm[:, 0:1], None,
                                        ALU.mult).then_inc(top2_step, 1)
                dve.wait_ge(top2_step, base + 1)
                nc.vector.scalar_tensor_tensor(out=logits[:], in0=logit_ps[:, LOGITS:LOGITS + E], scalar=inv_norm[:, 0:1],
                                               in1=logit_lo[:], op0=ALU.mult, op1=ALU.add).then_inc(logits_ready, 1)
                wait_apart(dve, dve_passed, logits_ready, n + 1)
                nc.vector.max(out=top[:], in_=logits[:]).then_inc(top2_step, 1)
                wait_apart(dve, dve_passed, top2_step, base + 2)
                nc.vector.max_index(top_at[:], top[:], logits[:]).then_inc(top2_step, 1)
                dve.wait_ge(top2_step, base + 3)
                nc.vector.tensor_tensor(gap[:], top[:, 1:2], top[:, 0:1], ALU.subtract).then_inc(top2_step, 1)
                nc.vector.tensor_copy(top_at_f[:], top_at[:, 0:2]).then_inc(top2_step, 1)
                dve.wait_ge(ratio_ready, n + 1)
                nc.vector.tensor_scalar(ratio_1[:], ratio[:], 1.0, None, ALU.add).then_inc(top2_step, 1)
                dve.wait_ge(top2_step, base + 6)
                nc.vector.reciprocal(weight[:, 0:1], ratio_1[:]).then_inc(top2_step, 1)
                dve.wait_ge(top2_step, base + 7)
                nc.vector.tensor_tensor(weight[:, 1:2], ratio[:], weight[:, 0:1], ALU.mult).then_inc(top2_step, 1)
                dve.wait_ge(top2_step, base + 8)
                nc.vector.tensor_scalar(combine_0[:], expert_no[:], top_at_f[:, 0:1], weight[:, 0:1],
                                        ALU.is_equal, ALU.mult)
                nc.vector.tensor_scalar(combine_1[:], expert_no[:], top_at_f[:, 1:2], weight[:, 1:2],
                                        ALU.is_equal, ALU.mult).then_inc(top2_step, 1)
                dve.wait_ge(top2_step, base + 9)
                nc.vector.tensor_tensor(combine[:], combine_0[:], combine_1[:], ALU.add).then_inc(top2_step, 1)
                dve.wait_ge(top2_step, base + 10)

            def scale_up(n):
                dve.wait_ge(up_mm, n + 1)
                wait(dve, s_transposed, NB * n)
                for j in range(NB):
                    last = nc.vector.tensor_tensor(
                        s_sb[:, cols(j, C)].rearrange("p (e r) -> p e r", r=R),
                        up_ps[j][:].rearrange("p (e r) -> p e r", r=R),
                        combine[:, j * EPB:(j + 1) * EPB].unsqueeze(2).broadcast_to((P, EPB, R)), ALU.mult)
                last.then_inc(s_ready, 1)

            def rest_of_s(n):
                for j in range(NB):
                    dve.wait_ge(sT_hi_ready, NB * n + j + 1)
                    last = nc.vector.tensor_tensor(sT_lo[:, j * EPB:(j + 1) * EPB, :],
                                                   sT_ps[j][:].rearrange("p (e t) -> p e t", t=P),
                                                   f32(sT_hi[:, j * EPB:(j + 1) * EPB, :]), ALU.subtract)
                last.then_inc(sT_lo_ready, 1)

            def gate_ffn(n):
                dve.wait_ge(ffn_mm, n + 1)
                wait(dve, out_ready, n)
                nc.vector.tensor_tensor(ffn[:], ffn_ps[:], mods[:, GB, n // TB, :], ALU.mult).then_inc(ffn_ready, 1)

            def step(i, has_prev, has_next, has_second, has_third):
                top2(i)
                scale_up(i)
                if has_next:
                    add_attention(i + 1)
                    norm_2(i + 1, i + 2 if has_second else None)
                if has_prev:
                    gate_ffn(i - 1)
                if has_next:
                    rest_of_hT(NT + i + 1)
                if has_third:
                    normalise_q(i + 3)
                rest_of_s(i)

            dve.wait_ge(ksum_ready, 1)
            normalise_q(0)
            phi_k(NT - 1)
            rest_of_qz(0)
            phi_q(NT - 1)
            normalise_q(1)
            mask_kv(1)
            add_attention(0)
            norm_2(0, 1)
            rest_of_m(1, range(KC // 2))
            rest_of_hT(NT)
            rest_of_m(1, range(KC // 2, KC))
            add_attention(1)
            norm_2(1)
            top2(0)
            scale_up(0)
            rest_of_hT(NT + 1)
            dve.wait_ge(ksum_ready, B)
            normalise_q(2)
            rest_of_s(0)
            top2(1)
            rest_of_qz(2)
            normalise_q(3)
            add_attention(2)
            norm_2(2)
            rest_of_qz(3)
            scale_up(1)
            gate_ffn(0)
            rest_of_hT(NT + 2)
            normalise_q(4)
            rest_of_s(1)
            with dve.Fori(2, NT - 3) as i:
                step(i, True, True, True, True)
            for i in range(NT - 3, NT):
                step(i, True, i + 1 < NT, i + 2 < NT, i + 3 < NT)
            wait(dve, out_ready, NT - 1)
            for g in range(2):
                half = cols(g, C // 2)
                dve.wait_ge(ffn_mm, NT + g)
                nc.vector.tensor_tensor(ffn[:, half], last_ps[g][:, half], mods[:, GB, B - 1, half], ALU.mult).then_inc(ffn_ready, 1)
                dve.wait_ge(ffn_ready, NT + g)
                nc.vector.tensor_tensor(xq[:, NT - 1, half], xq[:, NT - 1, half], ffn[:, half],
                                        ALU.add).then_inc(last_out_ready, 1)

        @block.tensor
        def _(pe):
            mm = nc.tensor.matmul

            def sum_mod(d, b):
                pe.wait_ge(mod_acc_ready, d + 1)
                mm(mod_ps[b][:], ones[:], mod_acc[b][:], start=True, stop=True).then_inc(mod_mm, 1)

            def sum_split_mods(d):
                pe.wait_ge(mod_ready, d + B)
                pe.wait_ge(mod_hi_ready, d)
                for b in range(B):
                    mm(mod_ps[b][:], ones_r[:], mod_acc_hi[b][:], start=True, stop=False)
                for b in range(B):
                    pe.wait_ge(mod_lo_ready, d + b + 1 - B)
                    mm(mod_ps[b][:], ones_r[:], mod_acc_lo[b][:], start=False, stop=True).then_inc(mod_mm, 1)

            def mod_direct(n, chunks, arrived):
                for k in chunks:
                    if k % (KC // 2) == 0:
                        pe.wait_ge(arrived[k // (KC // 2)], 16)
                    last = mm(direct_ps[n][:], silu_wide[:, k, :], wmod_raw[:, n, k, :], start=(k == 0), stop=(k == KC - 1))
                return last

            def transpose_h(m):
                pe.wait_ge(h_ready, m + 1)
                for k in range(KC):
                    last = nc.tensor.transpose(hT_ps[:, cols(k)], h[:, cols(k)], ident[:])
                last.then_inc(h_transposed, 1)

            def project(dst, hi, lo, w_hi_of, w_lo_of, second_half=None, lo_ready=None, w_lo_ready=None):
                passes = [(hi, w_hi_of, None), (hi, w_lo_of, w_lo_ready), (lo, w_hi_of, lo_ready)]
                if w_lo_ready is not None:
                    passes = [passes[0], passes[2], passes[1]]
                for part, w_of, ready in passes:
                    if ready is not None:
                        pe.wait_ge(*ready)
                    for k in range(KC):
                        if k == KC // 2 and second_half is not None:
                            pe.wait_ge(*second_half)
                            second_half = None
                        last = mm(dst, part[:, cols(k)], w_of(k), start=(part is hi and w_of is w_hi_of and k == 0),
                                  stop=(part is passes[2][0] and w_of is passes[2][1] and k == KC - 1))
                return last

            def project_h(j, dst, **ready):
                return project(dst[:], hT_hi, hT_lo, lambda k: w_hi[:, j, k, :], lambda k: w_lo[:, j, k, :], **ready)

            pe.wait_ge(const_ready, CONSTANTS)
            pe.wait_ge(silu_wide_ready, 1)
            mod_direct(CA, range(KC // 2), ca_in)
            sum_mod(0, 0)
            mod_direct(CA, range(KC // 2, KC - 1), ca_in)
            sum_mod(1, 1)
            mod_direct(CA, range(KC - 1, KC), ca_in).then_inc(mod_mm, 1)
            mod_direct(SA, range(KC // 2), sa_in)
            pe.wait_ge(ident_ready, 1)
            transpose_h(0)
            mod_direct(SA, range(KC // 2, KC), sa_in).then_inc(mod_mm, 1)

            def times_k(i):
                pe.wait_ge(hT_hi_ready, 2 * i + 1)
                wait(pe, k_parts, i)
                first = isinstance(i, int) and i == 0
                if first:
                    pe.wait_ge(w_hi_ready, 1)
                project_h(K, k_ps, second_half=(hT_hi_ready, 2 * i + 2), lo_ready=(hT_lo_ready, i + 1), w_lo_ready=(w_lo_ready, 1) if first else None).then_inc(k_mm, 1)

            def times_v(i):
                wait(pe, v_ready, i)
                first = isinstance(i, int) and i == 0
                if first:
                    pe.wait_ge(w_hi_ready, 2)
                project_h(V, v_ps, w_lo_ready=(w_lo_ready, 2) if first else None).then_inc(v_mm, 1)

            def times_q(i):
                wait(pe, q_parts, i)
                first = isinstance(i, int) and i == 0
                if first:
                    pe.wait_ge(w_hi_ready, 3)
                project_h(Q, q_ps, w_lo_ready=(w_lo_ready, 3) if first else None).then_inc(q_mm, 1)

            def add_kv(i, t):
                pe.wait_ge(k_ready, i + 1)
                pe.wait_ge(v_ready, i + 1)
                if t == 0:
                    pe.wait_ge(mod_ready, 4)
                    wait(pe, kv_ready, i // TB)
                    wait(pe, m_ready, i // TB * KC)
                for j in range(KC):
                    last = mm(kv_ps[:, cols(j)], v_sb[:, cols(j)], k_sb[:, cols(j)],
                              start=(t == 0 and j == 0), stop=(t == TB - 1), skip_group_check=True)
                last.then_inc(kv_mm, 1)

            def rest_of_tile(i, t=None, d=None):
                if d is not None:
                    sum_split_mods(d)
                times_v(i)
                transpose_h(i + 1)
                if isinstance(i, int) and i == TB:
                    pe.wait_ge(m_ready, KC)
                times_q(i)
                add_kv(i, t)

            def tile(i, t=None, d=None):
                times_k(i)
                rest_of_tile(i, t, d)

            def sum_k(b):
                pe.wait_ge(k_added, (b + 1) * TB)
                wait(pe, ksum_ready, b)
                mm(ksum_ps[:], ones[:], k_acc[:], start=True, stop=True).then_inc(ksum_mm, 1)

            def make_m(b):
                pe.wait_ge(wo_gated, b + 1)
                pe.wait_ge(q_parts, (b + 1) * TB)
                pe.wait_ge(v_ready, (b + 1) * TB)
                pe.wait_ge(kv_ready, b + 1)
                wait(pe, m_ready, b * KC)
                for j in range(KC):
                    mm(m_ps[b][j][:], kv_sb[:, cols(j)], wo_f[:, j, :], start=True, stop=True).then_inc(m_mm, 1)

            times_k(0)
            times_v(0)
            times_q(0)
            transpose_h(1)
            add_kv(0, 0)
            tile(1)
            with pe.Fori(2, 6) as t:
                tile(t, None, B * (t - 1))
            tile(TB - 2)
            tile(TB - 1, TB - 1)
            sum_k(0)
            times_k(TB)
            make_m(0)
            rest_of_tile(TB, 0)
            with pe.Fori(TB + 1, NT - 1) as i:
                tile(i)

            def transpose_qz(n, bank_read):
                pe.wait_ge(qz_ready, n + 1)
                if bank_read is not None:
                    pe.wait_ge(*bank_read)
                for k in range(KC):
                    last = nc.tensor.transpose(t_ps[:, cols(k)], qz[:, cols(k)], ident[:])
                last.then_inc(qz_transposed, 1)

            def attention(n):
                b = n // TB
                pe.wait_ge(qzT_hi_ready, n + 1)
                wait(pe, x1_ready, n)
                project(attn_ps[:], qzT_hi, qzT_lo, lambda k: m_hi[:, b, k, :], lambda k: m_lo[:, b, k, :],
                        lo_ready=(qzT_lo_ready, n + 1)).then_inc(attn_mm, 1)

            def experts_up(i, midway=None):
                pe.wait_ge(hT_hi_ready, 2 * (NT + i) + 1)
                wait(pe, logits_ready, i)
                wait(pe, s_ready, i)
                for k in range(KC):
                    if k == KC // 2:
                        pe.wait_ge(hT_hi_ready, 2 * (NT + i) + 2)
                    for j in range(NB):
                        mm(up_ps[j][:], hT_hi[:, cols(k)], wa_hi[:, k, cols(j, C)], start=(k == 0), stop=False)
                        mm(up_ps[j][:], hT_hi[:, cols(k)], wa_lo[:, k, cols(j, C)], start=False, stop=False)
                    if k == 1:
                        pe.wait_ge(hT_lo_ready, NT + i + 1)
                        for c in range(KC):
                            for part in (hT_hi, hT_lo):
                                last = mm(logit_ps[0:2 * E, 0:P], router_2[:, c, :], part[:, cols(c)],
                                          start=(c == 0 and part is hT_hi), stop=(c == KC - 1 and part is hT_lo))
                        last.then_inc(logit_T_mm, 1)
                        if midway is not None:
                            midway()
                    if k == 2:
                        wait_apart(pe, pe_passed, logits_T_ready, i + 1)
                        nc.tensor.transpose(logit_ps[:, LOGITS:LOGITS + 2 * E], logits_T[:], ident[0:2 * E, 0:2 * E]).then_inc(logit_mm, 1)
                for k in range(KC):
                    for j in range(NB):
                        last = mm(up_ps[j][:], hT_lo[:, cols(k)], wa_hi[:, k, cols(j, C)], start=False, stop=(k == KC - 1))
                last.then_inc(up_mm, 1)

            def experts_down(n, midway=None):
                wait(pe, ffn_ready, n)
                for e in range(E):
                    if e % EPB == 0:
                        pe.wait_ge(sT_hi_ready, NB * n + e // EPB + 1)
                    mm(ffn_ps[:], sT_hi[:, e, :], wb_hi[:, e, :], start=(e == 0), stop=False)
                    mm(ffn_ps[:], sT_hi[:, e, :], wb_lo[:, e, :], start=False, stop=False)
                if midway is not None:
                    midway()
                pe.wait_ge(sT_lo_ready, n + 1)
                for e in range(E):
                    last = mm(ffn_ps[:], sT_lo[:, e, :], wb_hi[:, e, :], start=False, stop=(e == E - 1))
                last.then_inc(ffn_mm, 1)

            def transpose_s(i):
                pe.wait_ge(s_ready, i + 1)
                wait(pe, sT_lo_ready, i)
                for e in range(E):
                    last = nc.tensor.transpose(sT_ps[e // EPB][:, cols(e % EPB)], s_sb[:, cols(e)], ident[:])
                    if e % EPB == EPB - 1:
                        last.then_inc(s_transposed, 1)

            def first_steps():
                experts_up(0)
                transpose_h(NT + 1)
                transpose_s(0)
                experts_up(1, midway=lambda: transpose_qz(2, None))
                attention(2)
                pe.wait_ge(wb_ready, 2)
                experts_down(0, midway=lambda: transpose_qz(3, (qzT_lo_ready, 3)))
                pe.wait_ge(qzT_lo_ready, 4)
                transpose_h(NT + 2)
                transpose_s(1)

            def step(i, has_prev, has_next, has_second):
                experts_up(i)
                if has_second:
                    transpose_qz(i + 2, (hT_lo_ready, NT + i + 1))
                if has_next:
                    attention(i + 1)
                if has_prev:
                    experts_down(i - 1)
                if has_next:
                    if has_second:
                        pe.wait_ge(qzT_lo_ready, i + 3)
                    transpose_h(NT + i + 1)
                transpose_s(i)

            times_k(NT - 1)
            times_v(NT - 1)
            transpose_qz(0, (hT_lo_ready, NT))
            times_q(NT - 1)
            add_kv(NT - 1, TB - 1)
            sum_k(1)
            pe.wait_ge(m_ready, KC)
            pe.wait_ge(q_parts, NT)
            attention(0)
            transpose_qz(1, (qzT_lo_ready, 1))
            make_m(1)
            pe.wait_ge(qzT_lo_ready, 2)
            transpose_h(NT)
            attention(1)
            pe.wait_ge(router_ready, 1)
            pe.wait_ge(wa_ready, TB)
            pe.wait_ge(m_ready, B * KC)
            first_steps()
            with pe.Fori(2, NT - 3) as i:
                step(i, True, True, True)
            for i in range(NT - 3, NT):
                step(i, True, i + 1 < NT, i + 2 < NT)
            n = NT - 1
            pe.wait_ge(ffn_ready, n)
            for g in range(2):
                half = cols(g, C // 2)
                for e in range(E):
                    if g == 0 and e % EPB == 0:
                        pe.wait_ge(sT_hi_ready, NB * n + e // EPB + 1)
                    mm(last_ps[g][:, half], sT_hi[:, e, :], wb_hi[:, e, half], start=(e == 0), stop=False)
                    mm(last_ps[g][:, half], sT_hi[:, e, :], wb_lo[:, e, half], start=False, stop=False)
                if g == 0:
                    pe.wait_ge(sT_lo_ready, n + 1)
                for e in range(E):
                    last = mm(last_ps[g][:, half], sT_lo[:, e, :], wb_hi[:, e, half], start=False, stop=(e == E - 1))
                last.then_inc(ffn_mm, 1)


def kernel(L0_attn_x, L0_attn_cos, L0_attn_sin, L0_attn_Wq, L0_attn_Wk, L0_attn_Wv, L0_attn_Wo,
           L0_ffn_router_w, L0_ffn_Wa, L0_ffn_Wb, L0_c, L0_wmod):
    import concourse.bacc as bacc
    import numpy as np
    from concourse.bass_utils import run_bass_kernel_spmd

    def dense(a):
        return np.ascontiguousarray(a)

    x = np.asarray(L0_attn_x)
    c = np.asarray(L0_c)
    experts, features, rank = L0_ffn_Wa.shape
    chunks = features // P
    arrays = {
        "x": dense(x.reshape(-1, features)),
        "c_cols": dense(c.T.reshape(chunks, P, -1).transpose(1, 0, 2)),
        "wq": dense(np.asarray(L0_attn_Wq).T),
        "wk": dense(np.asarray(L0_attn_Wk).T),
        "wv": dense(np.asarray(L0_attn_Wv).T),
        "wo": dense(np.asarray(L0_attn_Wo).T),
        "router": dense(np.asarray(L0_ffn_router_w).reshape(chunks, P, -1).transpose(1, 0, 2)),
        "wa": dense(np.asarray(L0_ffn_Wa).transpose(1, 0, 2).reshape(features, experts * rank)),
        "wb": dense(L0_ffn_Wb),
        "wmod": dense(L0_wmod),
    }
    nc = bacc.Bacc("TRN2", target_bir_lowering=False, num_devices=1)
    args = [nc.dram_tensor(name, a.shape, mybir.dt.from_np(a.dtype), kind="ExternalInput").ap()
            for name, a in arrays.items()]
    out = nc.dram_tensor("out", arrays["x"].shape, F32, kind="ExternalOutput").ap()
    adaln_block(nc, *args, out)
    result = run_bass_kernel_spmd(nc, [arrays], core_ids=[0])
    return result.results[0]["out"].reshape(x.shape)
```
